# Optimizing a Trainium2 kernel written in Bass

```python
import numpy as np
import jax
import jax.numpy as jnp

def _softmax(x, axis=-1):
    return jax.nn.softmax(x, axis=axis)

def _gelu(x):
    return jax.nn.gelu(x, approximate=True)

def _silu(x):
    return jax.nn.silu(x)

def _sigmoid(x):
    return jax.nn.sigmoid(x)

def _layernorm(x, axis=-1, eps=1e-05):
    m = jnp.mean(x, axis=axis, keepdims=True)
    v = jnp.var(x, axis=axis, keepdims=True)
    return (x - m) / jnp.sqrt(v + eps)

def _scatter_add(tgt, idx, src, axis=0):
    return tgt.at[idx].add(src)

def _segment_sum(src, seg, n):
    return jax.ops.segment_sum(src, seg, n)
kernel_name = 'mk_flamingo_gated_d1_seqx_r8_9ce867'

def setup_inputs(seed: int=0):
    np.random.seed(seed)
    _w = jnp.asarray

    def _rec_inputs():
        import jax
        import jax.numpy as jnp
        _rk = jax.random.key(seed)
        x = -0.0002928 + 1 * jax.random.normal(jax.random.fold_in(_rk, 1), (16, 64, 128), jnp.float32)
        _lenS = 64 - jax.random.randint(jax.random.fold_in(_rk, 7), (16,), 0, max(1, 64 // 4) + 1, jnp.int32)
        _lenS2 = 64 - jax.random.randint(jax.random.fold_in(_rk, 8), (16,), 0, max(1, 64 // 4) + 1, jnp.int32)
        _ctx_1024P = jax.random.normal(jax.random.fold_in(_rk, 11), (16, 16, 128), jnp.float32)
        _ctx_1024c = jax.random.dirichlet(jax.random.fold_in(_rk, 511), 0.3 * jnp.ones((16,), jnp.float32), (16, 64))
        _ctx_1024t = jnp.einsum('bsk,bkd->bsd', _ctx_1024c, _ctx_1024P)
        _ctx_1024t = _ctx_1024t * jax.lax.rsqrt(jnp.mean(jnp.square(_ctx_1024t)) + 1e-12) * 0.953939
        ctx_1024 = -1.39393e-06 + 0.999914 * (_ctx_1024t + 0.3 * jax.random.normal(jax.random.fold_in(_rk, 611), (16, 64, 128), jnp.float32))
        _validS = jnp.arange(64)[None, :] < _lenS[:, None]
        _validS2 = jnp.arange(64)[None, :] < _lenS2[:, None]
        _causal = jnp.tril(jnp.ones((64, 64), dtype=bool))
        mask_BxS2_bf0 = jnp.logical_not(jnp.ones((16, 64), dtype=bool))
        _g = jax.random.normal(jax.random.fold_in(_rk, 9001), (2, 1), jnp.float32)
        _g = jnp.sign(_g) * jnp.maximum(jnp.abs(_g), 1.0) + (_g == 0) * 1.0
        g_xattn = _g[0]
        g_ffn = _g[1]
        return (x, ctx_1024, mask_BxS2_bf0, g_xattn, g_ffn)
    x, ctx_1024, mask_BxS2_bf0, g_xattn, g_ffn = _rec_inputs()

    def _L0_xattn_setup():
        import jax, jax.numpy as jnp
        import numpy as np
        B, SQ, SKV, D, H = (2, 256, 256, 128, 16)
        HD = D // H

        def cross_attention(query, context, mask, Wq, bq, Wkv, bkv, Wout, bout, num_heads):
            b, sq, d = query.shape
            skv = context.shape[1]
            hd = d // num_heads
            scale = hd ** (-0.5)
            q = query @ Wq + bq
            kv = context @ Wkv + bkv
            kv = kv.reshape(b, skv, 2, num_heads, hd).transpose(2, 0, 3, 1, 4)
            k, v = (kv[0], kv[1])
            q = q.reshape(b, sq, num_heads, hd).transpose(0, 2, 1, 3)
            scores = jnp.einsum('bhid,bhjd->bhij', q, k) * scale
            scores = jnp.where(mask[:, None, None, :], -jnp.inf, scores)
            attn = jax.nn.softmax(scores, axis=-1)
            out = jnp.einsum('bhij,bhjd->bhid', attn, v)
            out = out.transpose(0, 2, 1, 3).reshape(b, sq, d)
            return out @ Wout + bout
        key = jax.random.key(seed)
        ks = jax.random.split(key, 6)
        scale = 1.0 / np.sqrt(D)
        return {'query': jax.random.normal(ks[0], (B, SQ, D), dtype=jnp.float32), 'context': jax.random.normal(ks[1], (B, SKV, D), dtype=jnp.float32), 'mask': jnp.zeros((B, SKV), dtype=bool), 'Wq': jax.random.normal(ks[2], (D, D), dtype=jnp.float32) * scale, 'bq': jnp.zeros((D,), dtype=jnp.float32), 'Wkv': jax.random.normal(ks[3], (D, 2 * D), dtype=jnp.float32) * scale, 'bkv': jnp.zeros((2 * D,), dtype=jnp.float32), 'Wout': jax.random.normal(ks[4], (D, D), dtype=jnp.float32) * scale, 'bout': jnp.zeros((D,), dtype=jnp.float32), 'num_heads': H}
    _L0_xattn_all = _L0_xattn_setup()
    _L0_xattn_in = {k: v for k, v in _L0_xattn_all.items() if k in ('Wq', 'bq', 'Wkv', 'bkv', 'Wout', 'bout')}
    del _L0_xattn_all

    def _L0_ffn_setup():
        import jax, jax.numpy as jnp
        import numpy as np
        B, T, C = (8, 256, 128)
        H = 512
        E = 8
        K = 2
        LOAD_FACTOR = 1.2
        N_LAYER = 12

        def _get_expert_inputs(x, logits, expert_capacity):
            Tt = logits.shape[0]
            Cc = x.shape[1]
            top_k_logits, expert_indices = jax.lax.top_k(logits, K)
            expert_probs = jax.nn.softmax(top_k_logits, axis=-1)
            ei = jnp.swapaxes(expert_indices, 0, 1).ravel()
            one_hot = jax.nn.one_hot(ei, E, dtype=jnp.int32)
            pos = jnp.cumsum(one_hot, axis=0) * one_hot - 1
            pos = pos.reshape(-1, Tt, E)
            pos = jnp.swapaxes(pos, 0, 1)
            pos = jnp.max(pos, axis=2)
            ei = jnp.swapaxes(ei.reshape(-1, Tt), 0, 1)
            buf = jnp.zeros((E, expert_capacity, Cc), x.dtype)
            xr = jnp.repeat(x, K, axis=0)
            expert_inputs = buf.at[ei.ravel(), pos.ravel()].add(xr)
            return (expert_probs, pos, ei, expert_inputs)
        key = jax.random.key(seed)
        ks = jax.random.split(key, 9)
        std = 0.02
        proj_std = 0.02 * (2 * N_LAYER) ** (-0.5)
        return {'x': jax.random.normal(ks[0], (B, T, C), jnp.float32), 'router_w': jax.random.normal(ks[1], (C, E), jnp.float32) * std, 'router_b': jnp.zeros((E,), jnp.float32), 'w_c_fc': jax.random.normal(ks[2], (E, C, H), jnp.float32) * std, 'b_c_fc': jnp.zeros((E, 1, H), jnp.float32), 'w_gate': jax.random.normal(ks[3], (E, C, H), jnp.float32) * std, 'b_gate': jnp.zeros((E, 1, H), jnp.float32), 'w_c_proj': jax.random.normal(ks[4], (E, H, C), jnp.float32) * proj_std, 'b_c_proj': jnp.zeros((E, 1, C), jnp.float32)}
    _L0_ffn_all = _L0_ffn_setup()
    _L0_ffn_in = {k: v for k, v in _L0_ffn_all.items() if k in ('router_w', 'router_b', 'w_c_fc', 'b_c_fc', 'w_gate', 'b_gate', 'w_c_proj', 'b_c_proj')}
    del _L0_ffn_all
    return {'x': x, 'ctx_1024': ctx_1024, 'mask_BxS2_bf0': mask_BxS2_bf0, 'g_xattn': g_xattn, 'g_ffn': g_ffn, 'L0_xattn_Wq': _L0_xattn_in['Wq'], 'L0_xattn_bq': _L0_xattn_in['bq'], 'L0_xattn_Wkv': _L0_xattn_in['Wkv'], 'L0_xattn_bkv': _L0_xattn_in['bkv'], 'L0_xattn_Wout': _L0_xattn_in['Wout'], 'L0_xattn_bout': _L0_xattn_in['bout'], 'L0_ffn_router_w': _L0_ffn_in['router_w'], 'L0_ffn_router_b': _L0_ffn_in['router_b'], 'L0_ffn_w_c_fc': _L0_ffn_in['w_c_fc'], 'L0_ffn_b_c_fc': _L0_ffn_in['b_c_fc'], 'L0_ffn_w_gate': _L0_ffn_in['w_gate'], 'L0_ffn_b_gate': _L0_ffn_in['b_gate'], 'L0_ffn_w_c_proj': _L0_ffn_in['w_c_proj'], 'L0_ffn_b_c_proj': _L0_ffn_in['b_c_proj']}

def reference(x, ctx_1024, mask_BxS2_bf0, g_xattn, g_ffn, L0_xattn_Wq, L0_xattn_bq, L0_xattn_Wkv, L0_xattn_bkv, L0_xattn_Wout, L0_xattn_bout, L0_ffn_router_w, L0_ffn_router_b, L0_ffn_w_c_fc, L0_ffn_b_c_fc, L0_ffn_w_gate, L0_ffn_b_gate, L0_ffn_w_c_proj, L0_ffn_b_c_proj):
    import jax
    import jax.numpy as jnp

    def _L0_xattn_ref(query, context, mask, Wq, bq, Wkv, bkv, Wout, bout, num_heads):
        import jax, jax.numpy as jnp
        import numpy as np
        B, SQ, SKV, D, H = (2, 256, 256, 128, 16)
        HD = D // H

        def cross_attention(query, context, mask, Wq, bq, Wkv, bkv, Wout, bout, num_heads):
            b, sq, d = query.shape
            skv = context.shape[1]
            hd = d // num_heads
            scale = hd ** (-0.5)
            q = query @ Wq + bq
            kv = context @ Wkv + bkv
            kv = kv.reshape(b, skv, 2, num_heads, hd).transpose(2, 0, 3, 1, 4)
            k, v = (kv[0], kv[1])
            q = q.reshape(b, sq, num_heads, hd).transpose(0, 2, 1, 3)
            scores = jnp.einsum('bhid,bhjd->bhij', q, k) * scale
            scores = jnp.where(mask[:, None, None, :], -jnp.inf, scores)
            attn = jax.nn.softmax(scores, axis=-1)
            out = jnp.einsum('bhij,bhjd->bhid', attn, v)
            out = out.transpose(0, 2, 1, 3).reshape(b, sq, d)
            return out @ Wout + bout
        return cross_attention(query, context, mask, Wq, bq, Wkv, bkv, Wout, bout, num_heads)

    def _L0_ffn_ref(x, router_w, router_b, w_c_fc, b_c_fc, w_gate, b_gate, w_c_proj, b_c_proj):
        import jax, jax.numpy as jnp
        import numpy as np
        B, T, C = (8, 256, 128)
        H = 512
        E = 8
        K = 2
        LOAD_FACTOR = 1.2
        N_LAYER = 12

        def _get_expert_inputs(x, logits, expert_capacity):
            Tt = logits.shape[0]
            Cc = x.shape[1]
            top_k_logits, expert_indices = jax.lax.top_k(logits, K)
            expert_probs = jax.nn.softmax(top_k_logits, axis=-1)
            ei = jnp.swapaxes(expert_indices, 0, 1).ravel()
            one_hot = jax.nn.one_hot(ei, E, dtype=jnp.int32)
            pos = jnp.cumsum(one_hot, axis=0) * one_hot - 1
            pos = pos.reshape(-1, Tt, E)
            pos = jnp.swapaxes(pos, 0, 1)
            pos = jnp.max(pos, axis=2)
            ei = jnp.swapaxes(ei.reshape(-1, Tt), 0, 1)
            buf = jnp.zeros((E, expert_capacity, Cc), x.dtype)
            xr = jnp.repeat(x, K, axis=0)
            expert_inputs = buf.at[ei.ravel(), pos.ravel()].add(xr)
            return (expert_probs, pos, ei, expert_inputs)
        Bb, Tt, Cc = x.shape
        logits = jnp.einsum('btc,ce->bte', x, router_w) + router_b
        cap = int(LOAD_FACTOR * K * Tt // E)
        probs, pos, idx, einp = jax.vmap(lambda xb, lb: _get_expert_inputs(xb, lb, cap))(x, logits)
        if Bb % E == 0:
            t = einp.reshape(E, Bb // E, E, cap, Cc)
            t = jnp.swapaxes(t, 0, 2)
        else:
            t = jnp.swapaxes(einp, 0, 1)
        einp2 = t.reshape(E, Bb * cap, Cc)
        h = jnp.einsum('eti,eih->eth', einp2, w_c_fc) + b_c_fc
        g = jnp.einsum('eti,eih->eth', einp2, w_gate) + b_gate
        o = jnp.einsum('eth,eho->eto', jax.nn.silu(h * g), w_c_proj) + b_c_proj
        if Bb % E == 0:
            o = o.reshape(E, Bb // E, E, cap, Cc)
            o = jnp.swapaxes(o, 0, 2)
            o = o.reshape(Bb, E, cap, Cc)
        else:
            o = o.reshape(E, Bb, cap, Cc)
            o = jnp.swapaxes(o, 0, 1)

        def collect(eo, i, p, pr):
            sel = eo[i, p]
            return jnp.sum(pr[..., None] * sel, axis=1)
        return jax.vmap(collect)(o, idx, pos, probs)
    x = x + jnp.tanh(g_xattn[0]) * _L0_xattn_ref(_layernorm(x, axis=-1), ctx_1024, mask_BxS2_bf0, L0_xattn_Wq, L0_xattn_bq, L0_xattn_Wkv, L0_xattn_bkv, L0_xattn_Wout, L0_xattn_bout, 16)
    x = x + jnp.tanh(g_ffn[0]) * _L0_ffn_ref(_layernorm(x, axis=-1), L0_ffn_router_w, L0_ffn_router_b, L0_ffn_w_c_fc, L0_ffn_b_c_fc, L0_ffn_w_gate, L0_ffn_b_gate, L0_ffn_w_c_proj, L0_ffn_b_c_proj)
    return x

_drawn_inputs = setup_inputs


def setup_inputs(seed=0):
    import zlib

    import numpy as np

    out = dict(_drawn_inputs(seed))
    spreads = {'L0_xattn_bq': (0.0, 0.387),
     'L0_xattn_bkv': (0.0, 0.1),
     'L0_xattn_bout': (0.0, 0.1),
     'L0_ffn_router_b': (0.0, 0.1),
     'L0_ffn_b_c_fc': (0.0, 0.8),
     'L0_ffn_b_gate': (0.0, 0.8),
     'L0_ffn_b_c_proj': (0.0, 0.1)}
    factors = {'L0_ffn_w_c_fc': 8.0, 'L0_ffn_w_gate': 8.0, 'L0_ffn_w_c_proj': 8.0}
    for name, (base, spread) in spreads.items():
        noise = np.random.default_rng([zlib.crc32(name.encode()), seed]).standard_normal(out[name].shape)
        drawn = base * np.exp(spread * noise) if base else spread * noise
        out[name] = jnp.asarray(drawn.astype(out[name].dtype))
    for name, factor in factors.items():
        out[name] = (out[name] * factor).astype(out[name].dtype)
    return out
```

```python
from contextlib import ExitStack

import concourse.bass as bass
from concourse import mybir

F32 = mybir.dt.float32
BF16 = mybir.dt.bfloat16
U8 = mybir.dt.uint8
U32 = mybir.dt.uint32
ALU = mybir.AluOpType
ACT = mybir.ActivationFunctionType
AX_X = mybir.AxisListType.X

EPS = 1e-5
MASKED = -1.0e30
LOAD_FACTOR = 1.2
TOP_K = 2


def gated_attention_moe(nc, x, ctx_in, mask, g_xattn, g_ffn, wq, bq, wkv, bkv, wout, bout,
                        router_w, router_b, w_fc, b_fc, w_gate, b_gate, w_proj, b_proj, out):
    B, T, C = x.shape
    E = router_w.shape[1]
    F = w_fc.shape[2]
    H = 16
    D = C // H
    CAP = int(LOAD_FACTOR * TOP_K * T // E)
    P = 2 * T
    NP = B // 2
    HALF = C // 2
    HH = H // 2
    FC = F // 128
    SLOTS = 2 * CAP
    PS = E * SLOTS
    ES = B * CAP
    GROUPS = [(0, 3), (3, 3), (6, 2)]
    GW = 3 * SLOTS
    SCALE = float(D) ** -0.5
    assert P == 128 and C == 128 and D == 8 and NP == 8 and E == 8

    with ExitStack() as stack:
        def sb(name, shape, dt=F32):
            return stack.enter_context(nc.sbuf_tensor(name, shape, dt))

        def ps(name, shape):
            return stack.enter_context(nc.psum_tensor(name, shape, F32))

        def sem(name):
            return stack.enter_context(nc.semaphore(name))

        x_sb = sb("x_sb", [P, NP, C])
        c_sb = sb("c_sb", [P, NP, C])
        xn = sb("xn", [P, NP, C])
        xnT = sb("xnT", [C, NP * P])
        cT = sb("cT", [C, NP * P])
        wq_sb = sb("wq_sb", [C, C])
        wkv_sb = sb("wkv_sb", [C, 2 * C])
        wout_sb = sb("wout_sb", [C, C])
        b_rows = sb("b_rows", [77, 128])
        bT = sb("bT", [128, 77])
        bq_sb, bk_sb, bv_sb = bT[:, 72:74], bT[:, 74:76], bT[:, 76:77]
        bout_bc = sb("bout_bc", [P, C])
        gx = sb("gx", [P, 1])
        gf = sb("gf", [P, 1])
        tgx = sb("tgx", [P, 1])
        tgf = sb("tgf", [P, 1])
        rw_sb = sb("rw_sb", [C, E])
        rb_bc = sb("rb_bc", [P, E])
        mask_nat = sb("mask_nat", [P, NP, T], U8)
        mask_u8 = sb("mask_u8", [64, NP, T], U8)
        penalty = sb("penalty", [64, NP, T], BF16)
        batch_row = sb("batch_row", [64, P], BF16)
        nmask = sb("nmask", [P, NP])
        live = sb("live", [P, NP])
        rlive = sb("rlive", [P, NP])
        nanfix = sb("nanfix", [P, NP])
        wfc_sb = sb("wfc_sb", [C, E, F])
        wg_sb = sb("wg_sb", [C, E, F])
        wp_sb = sb("wp_sb", [128, E, FC, C])
        bfc_sb = bT[:, 0:E * FC].rearrange("p (e c) -> p e c", e=E)
        bg_sb = bT[:, E * FC:2 * E * FC].rearrange("p (e c) -> p e c", e=E)
        bp_sb = bT[:, 2 * E * FC:2 * E * FC + E]
        ident = sb("ident", [128, 128])
        hmask = sb("hmask", [P, HH])
        before = sb("before", [P, P], BF16)
        same = sb("same", [P, P], BF16)
        iota_e = sb("iota_e", [P, E])
        iota_s = sb("iota_s", [P, CAP])
        mhalf = sb("mhalf", [P, NP])
        stats = sb("stats", [P, NP, 6])
        mv = sb("mv", [P, NP, 2])
        veps = sb("veps", [P, NP])
        rstd = sb("rstd", [P, NP])
        stats2 = sb("stats2", [P, NP, 6])
        mv2 = sb("mv2", [P, NP, 2])
        veps2 = sb("veps2", [P, NP])
        rstd2 = sb("rstd2", [P, NP])
        qs = sb("qs", [P, 2, NP * T])
        ks = sb("ks", [P, 2 * NP * T])
        kbd = sb("kbd", [P, HH, 2 * NP * T])
        qbd = sb("qbd", [P, 2, 2, 2, T])
        vbd = sb("vbd", [P, B * HH * 32])
        pm = sb("pm", [P, 2, H, T])
        pn = sb("pn", [P, 2, H, T])
        negmax = sb("negmax", [P, NP, H])
        ssum = sb("ssum", [P, NP, H])
        rsum = sb("rsum", [P, NP, H])
        rsn = sb("rsn", [P, NP, H])
        pT = sb("pT", [P, 2, HH * P])
        aT = sb("aT", [C, 2, P])
        tb = sb("tb", [P, C])
        xb = sb("xb", [P, NP, C])
        x2 = sb("x2", [P, NP, C])
        xn2 = xn
        xn2T = sb("xn2T", [C, NP * P])
        lg = sb("lg", [P, NP, E])
        mx = sb("mx", [P, NP, 8])
        ix = sb("ix", [P, NP, 8], U32)
        idf = sb("idf", [P, 2, NP])
        oh = sb("oh", [P, 2, NP, E], BF16)
        pos0 = sb("pos0", [P, NP, E])
        pos1 = sb("pos1", [P, NP, E])
        slot = sb("slot", [P, NP, E])
        slotc = sb("slotc", [P, NP, E])
        dl = sb("dl", [P, NP])
        ex = sb("ex", [P, NP])
        den = sb("den", [P, NP])
        pr = sb("pr", [P, 2, NP])
        pw0 = sb("pw0", [P, NP, E])
        pw1 = sb("pw1", [P, NP, E])
        pw = sb("pw", [P, NP, E])
        disp = sb("disp", [P, NP, PS])
        coll = sb("coll", [P, NP, PS])
        kflat = kbd[:, :, :].rearrange("p h x -> p (h x)")
        collT = kflat[:, 0:3 * NP * P].rearrange("p (g n t) -> p g n t", g=3, n=NP)
        oT = kflat[:, 3 * NP * P:3 * NP * (P + GW)].rearrange("p (g n w) -> p g n w", g=3, n=NP)
        xe = vbd[:, 0:E * NP * SLOTS].rearrange("p (e n s) -> p e n s", e=E, n=NP)
        hs = sb("hs", [128, 2, ES])
        hg = sb("hg", [128, 2, ES])
        z = sb("z", [128, 3, ES])
        osl = sb("osl", [128, 2, 4, C])
        fin = c_sb

        pS = [ps(f"pS{r}", [128, 1024]) for r in range(2)]
        pT2 = ps("pT2", [128, 1024])
        p6 = ps("p6", [128, 512])
        p7 = ps("p7", [128, 512])
        BANKS = [pS[0][:, 0:512], pS[0][:, 512:1024], pS[1][:, 0:512], pS[1][:, 512:1024]]

        ld_x = sem("ld_x")
        ld_ctx = sem("ld_ctx")
        ld_wq = sem("ld_wq")
        ld_wkv = sem("ld_wkv")
        ld_bias = sem("ld_bias")
        ld_gate = sem("ld_gate")
        ld_mask = sem("ld_mask")
        ld_wout = sem("ld_wout")
        ld_router = sem("ld_router")
        bT_ps = sem("bT_ps")
        bT_ready = sem("bT_ready")
        ld_exp = [sem(f"ld_exp{e}") for e in range(E)]
        st_out = sem("st_out")
        pool_chain = sem("pool_chain")
        dve_chain = sem("dve_chain")
        c_ident = sem("c_ident")
        c_head = sem("c_head")
        c_pair = sem("c_pair")
        c_route = sem("c_route")
        c_zero = sem("c_zero")
        pen_ready = sem("pen_ready")
        var_ready = sem("var_ready")
        rstd_ready = sem("rstd_ready")
        xn_ready = sem("xn_ready")
        cT_ps = sem("cT_ps")
        cT_ready = sem("cT_ready")
        xT_ps = sem("xT_ps")
        xT_ready = sem("xT_ready")
        k_ps = sem("k_ps")
        k_ready = sem("k_ready")
        q_ps = sem("q_ps")
        q_ready = sem("q_ready")
        v_ps = sem("v_ps")
        v_ready = sem("v_ready")
        kbd_ready = sem("kbd_ready")
        qbd_ready = sem("qbd_ready")
        s_ps = sem("s_ps")
        shifted = sem("shifted")
        exped = sem("exped")
        rs_ready = sem("rs_ready")
        normed = sem("normed")
        pT_ps = sem("pT_ps")
        pT_ready = sem("pT_ready")
        o_ps = sem("o_ps")
        aT_ready = sem("aT_ready")
        y_ps = sem("y_ps")
        x2_ready = sem("x2_ready")
        xb_ready = sem("xb_ready")
        tg_ready = sem("tg_ready")
        var2_ready = sem("var2_ready")
        rstd2_ready = sem("rstd2_ready")
        xn2_ready = sem("xn2_ready")
        x2T_ps = sem("x2T_ps")
        x2T_ready = sem("x2T_ready")
        lg_ps = sem("lg_ps")
        oh_ready = sem("oh_ready")
        pos_ps = sem("pos_ps")
        dl_ready = sem("dl_ready")
        ex_ready = sem("ex_ready")
        disp_ready = sem("disp_ready")
        slot_ready = sem("slot_ready")
        coll_ready = sem("coll_ready")
        xe_ps = sem("xe_ps")
        xe_ready = sem("xe_ready")
        hg_ps = sem("hg_ps")
        h_ready = sem("h_ready")
        u_ready = sem("u_ready")
        z_ready = sem("z_ready")
        f_ps = sem("f_ps")
        oT_ready = sem("oT_ready")
        cT2_ps = sem("cT2_ps")
        collT_ready = sem("collT_ready")
        os_ps = sem("os_ps")
        os_ready = sem("os_ready")
        yf_ps = sem("yf_ps")
        fin_ready = sem("fin_ready")

        x_v = x.rearrange("(n a) i c -> (a i) n c", a=2)
        c_v = ctx_in.rearrange("(n a) i c -> (a i) n c", a=2)
        out_v = out.rearrange("(n a) i c -> (a i) n c", a=2)
        XH = NP // 2

        def row(v):
            return v.rearrange("(o c) -> o c", o=1)

        def link(eng, chain, count, ins):
            count[0] += 1
            ins.then_inc(chain, 1)
            eng.wait_ge(chain, count[0])

        block = stack.enter_context(nc.Block())

        @block.sync
        def _(sp):
            for h in range(2):
                sp.dma_start(x_sb[:, h * XH:(h + 1) * XH, :], x_v[:, h * XH:(h + 1) * XH, :]).then_inc(ld_x, 16)
            sp.dma_start(wq_sb[:, :], wq).then_inc(ld_wq, 16)
            sp.dma_start(b_rows[0:32, :], b_fc.rearrange("e o (c p) -> (e o c) p", p=128)).then_inc(ld_bias, 16)
            sp.dma_start(b_rows[32:64, :], b_gate.rearrange("e o (c p) -> (e o c) p", p=128)).then_inc(ld_bias, 16)
            sp.dma_start(b_rows[64:72, :], b_proj.rearrange("e o c -> (e o) c")).then_inc(ld_bias, 16)
            for a in range(2):
                sp.dma_start(b_rows[72:74, HALF * a:HALF * a + HALF],
                             bq.rearrange("(f r) -> f r", f=2)).then_inc(ld_bias, 16)
                sp.dma_start(b_rows[74:76, HALF * a:HALF * a + HALF],
                             bkv[0:C].rearrange("(f r) -> f r", f=2)).then_inc(ld_bias, 16)
            sp.dma_start(b_rows[76:77, :], row(bkv[C:2 * C])).then_inc(ld_bias, 16)
            sp.dma_start(wout_sb[:, :], wout).then_inc(ld_wout, 16)
            sp.dma_start(bout_bc[:, :], row(bout).broadcast_to([P, C])).then_inc(ld_gate, 16)
            sp.dma_start(gx[:, :], row(g_xattn).broadcast_to([P, 1])).then_inc(ld_gate, 16)
            sp.dma_start(gf[:, :], row(g_ffn).broadcast_to([P, 1])).then_inc(ld_gate, 16)
            sp.dma_start(rw_sb[:, :], router_w).then_inc(ld_router, 16)
            sp.dma_start(rb_bc[:, :], row(router_b).broadcast_to([P, E])).then_inc(ld_router, 16)
            for e in range(E):
                sp.dma_start(wfc_sb[:, e, :], w_fc[e]).then_inc(ld_exp[e], 16)
                sp.dma_start(wg_sb[:, e, :], w_gate[e]).then_inc(ld_exp[e], 16)
                sp.dma_start(wp_sb[:, e, :, :], w_proj[e].rearrange("(c p) o -> p c o", p=128)).then_inc(ld_exp[e], 16)
            for h in range(2):
                sp.wait_ge(fin_ready, h + 1)
                sp.dma_start(out_v[:, h * XH:(h + 1) * XH, :], fin[:, h * XH:(h + 1) * XH, :]).then_inc(st_out, 16)
            sp.wait_ge(st_out, 32)

        @block.gpsimd
        def _(pool):
            n = [0]
            g = nc.gpsimd

            def then(ins):
                link(pool, pool_chain, n, ins)

            then(g.memset(ident[:, :], 0.0))
            g.affine_select(out=ident[:, :], in_=ident[:, :], compare_op=ALU.not_equal, fill=1.0, base=0,
                            pattern=[[-1, 128]], channel_multiplier=1).then_inc(c_ident, 1)
            g.memset(mhalf[:, :], -0.5)
            then(g.memset(hmask[:, :], 1.0))
            for a in range(2):
                part = hmask[64 * a:64 * a + 64, :]
                then(g.affine_select(out=part, in_=part, compare_op=ALU.is_ge, fill=0.0, base=0,
                                     pattern=[[-D, HH]], channel_multiplier=1))
                then(g.affine_select(out=part, in_=part, compare_op=ALU.is_ge, fill=0.0, base=D - 1,
                                     pattern=[[D, HH]], channel_multiplier=-1))
            g.memset(vbd[:, 0:2048], 0.0).then_inc(c_head, 1)
            for h in range(2):
                lo, hi = h * XH, (h + 1) * XH
                pool.wait_ge(var_ready, h + 1)
                then(g.tensor_scalar(veps[:, lo:hi], mv[:, lo:hi, 1], EPS, None, ALU.add))
                g.tensor_tensor(rstd[:, lo:hi], veps[:, lo:hi], mhalf[:, lo:hi], ALU.pow).then_inc(rstd_ready, 1)
            g.memset(vbd[:, 2048:4096], 0.0).then_inc(c_zero, 1)
            then(g.memset(qbd[:, :, :, :, :], 0.0))
            then(g.memset(batch_row[:, :], 0.0))
            g.memset(batch_row[0:1, 0:T], 1.0).then_inc(c_pair, 1)
            pool.wait_ge(c_pair, 1)
            g.memset(batch_row[32:33, T:P], 1.0).then_inc(c_pair, 1)
            pool.wait_ge(c_pair, 2)
            pool.wait_ge(k_ready, 2)
            for h in range(6, 8):
                g.tensor_scalar(kbd[:, h, :], ks[:, :], hmask[:, h:h + 1], None, ALU.mult).then_inc(kbd_ready, 1)

            def queries(p):
                if p >= 2:
                    pool.wait_ge(s_ps, p - 1)
                for a in range(2):
                    g.tensor_copy(qbd[64 * a:64 * a + 64, p % 2, :, a, :],
                                  qs[64 * a:64 * a + 64, :, p * T:(p + 1) * T]).then_inc(qbd_ready, 1)
                    pool.wait_ge(qbd_ready, 2 * p + a + 1)

            pool.wait_ge(q_ready, 2)
            queries(0)
            queries(1)
            pool.wait_ge(tg_ready, 1)
            pool.wait_ge(ld_gate, 48)
            then(g.tensor_scalar(tb[:, :], bout_bc[:, :], tgx[:, 0:1], None, ALU.mult))
            g.tensor_tensor(xb[:, :, :], x_sb[:, :, :], tb[:, :].unsqueeze(1).broadcast_to([P, NP, C]),
                            ALU.add).then_inc(xb_ready, 1)
            for p in range(NP):
                pool.wait_ge(rs_ready, p + 1)
                if p >= 2:
                    pool.wait_ge(pT_ps, 2 * (p - 1))
                g.tensor_tensor(pn[:, p % 2, :, :], pm[:, p % 2, :, :],
                                rsn[:, p, :].unsqueeze(2).broadcast_to([P, H, T]), ALU.mult).then_inc(normed, 1)
                if p + 2 < NP:
                    queries(p + 2)
                if p == 0:
                    then(g.memset(before[:, :], 1.0))
                    then(g.affine_select(out=before[:, :], in_=before[:, :], compare_op=ALU.is_gt, fill=0.0,
                                         base=0, pattern=[[1, P]], channel_multiplier=-1))
                    g.memset(before[0:T, T:P], 0.0).then_inc(c_route, 1)
                    pool.wait_ge(c_route, 1)
                    then(g.memset(same[:, :], 1.0))
                    g.memset(same[0:T, T:P], 0.0).then_inc(c_route, 1)
                    pool.wait_ge(c_route, 2)
                    g.memset(same[T:P, 0:T], 0.0).then_inc(c_route, 1)
                    pool.wait_ge(c_route, 3)
                if p == 1:
                    g.iota(iota_e[:, :], [[1, E]], base=0, channel_multiplier=0,
                           allow_small_or_imprecise_dtypes=True).then_inc(c_route, 1)
                    g.iota(iota_s[:, :], [[1, CAP]], base=1, channel_multiplier=0,
                           allow_small_or_imprecise_dtypes=True).then_inc(c_route, 1)
                if p == 2:
                    g.memset(disp[:, :, :], 0.0).then_inc(c_route, 1)
                if p == 4:
                    g.memset(coll[:, :, :], 0.0).then_inc(c_zero, 1)
            pool.wait_ge(var2_ready, 1)
            then(g.tensor_scalar(veps2[:, :], mv2[:, :, 1], EPS, None, ALU.add))
            g.tensor_tensor(rstd2[:, :], veps2[:, :], mhalf[:, :], ALU.pow).then_inc(rstd2_ready, 1)
            for a in range(2):
                pool.wait_ge(slot_ready, a + 1)
                q = slice(64 * a, 64 * a + 64)
                cv = coll[q, :, :].rearrange("p n (e a s) -> p (n e) a s", a=2, s=CAP)[:, :, a, :]
                pv = pw[q, :, :].rearrange("p n e -> p (n e)").unsqueeze(2).broadcast_to([T, NP * E, CAP])
                g.tensor_tensor(cv, cv, pv, ALU.mult).then_inc(coll_ready, 1)
                pool.wait_ge(coll_ready, a + 1)

        @block.tensor
        def _(pe):
            mm = nc.tensor.matmul

            pe.wait_ge(c_ident, 1)
            for h in range(2):
                pe.wait_ge(ld_ctx, 16 * 2)
                for j in range(XH):
                    last = nc.tensor.transpose(pT2[:, 512 * h + 128 * j:512 * h + 128 * j + 128],
                                               c_sb[:, h * XH + j, :], ident[:, :])
                last.then_inc(cT_ps, 1)
            pe.wait_ge(ld_bias, 16 * 8)
            nc.tensor.transpose(p6[:, 0:77], b_rows[:, :], ident[0:77, 0:77]).then_inc(bT_ps, 1)
            pe.wait_ge(cT_ready, 2)
            pe.wait_ge(ld_wkv, 16)
            cTv = cT[:, :].rearrange("c (n a j) -> c a n j", a=2, j=T)
            for f in range(2):
                for a in range(2):
                    last = mm(BANKS[2 + f][64 * a:64 * a + 64, :], wkv_sb[:, HALF * f:HALF * f + HALF],
                              cTv[:, a], start=True, stop=True, tile_position=(0, 64 * a))
                last.then_inc(k_ps, 1)
            for h in range(2):
                pe.wait_ge(xn_ready, h + 1)
                for j in range(XH):
                    last = nc.tensor.transpose(pT2[:, 512 * h + 128 * j:512 * h + 128 * j + 128],
                                               xn[:, h * XH + j, :], ident[:, :])
                last.then_inc(xT_ps, 1)
            pe.wait_ge(bT_ready, 1)
            wv = wkv_sb[:, C:2 * C].rearrange("c (m s d) -> c s m d", s=2, d=D)
            for b in range(B):
                for s in range(2):
                    last = mm((p6, p7)[b // 8][64 * s:64 * s + 64, (b % 8) * 64:(b % 8) * 64 + 64],
                              cT[:, b * T:(b + 1) * T], wv[:, s], start=True, stop=True,
                              tile_position=(0, 64 * s))
                if b % 8 == 7:
                    last.then_inc(v_ps, 1)
            pe.wait_ge(xT_ready, 2)
            pe.wait_ge(ld_wq, 16)
            xTv = xnT[:, :].rearrange("c (n a j) -> c a n j", a=2, j=T)
            for f in range(2):
                for a in range(2):
                    last = mm(BANKS[f][64 * a:64 * a + 64, :], wq_sb[:, HALF * f:HALF * f + HALF],
                              xTv[:, a], start=True, stop=True, tile_position=(0, 64 * a))
                last.then_inc(q_ps, 1)

            kv = kbd[:, :, :].rearrange("p h (f n j) -> p f n h j", f=2, n=NP)

            def scores(p):
                if p < 2:
                    pe.wait_ge((q_ready, k_ready)[p], 2)
                else:
                    pe.wait_ge(shifted, p - 1)
                pe.wait_ge(qbd_ready, 2 * (p + 1))
                for f in range(2):
                    bank = pS[p % 2][:, 512 * f:512 * f + 512]
                    mm(bank, batch_row[:, :], penalty[:, p, :].unsqueeze(1).broadcast_to([64, HH, T]),
                       start=True, stop=False)
                    last = mm(bank, qbd[:, p % 2, f, :, :].rearrange("p a i -> p (a i)"), kv[:, f, p],
                              start=False, stop=True)
                last.then_inc(s_ps, 1)

            def transpose_probs(p):
                pe.wait_ge(normed, p + 1)
                for h in range(2):
                    if p == 0:
                        pe.wait_ge(xT_ready, 2)
                    else:
                        pe.wait_ge(pT_ready, 2 * (p - 1) + h + 1)
                    for m in range(4 * h, 4 * h + 4):
                        last = nc.tensor.transpose(
                            pT2[:, 128 * m:128 * m + 128],
                            pn[:, p % 2, 2 * m:2 * m + 2, :].rearrange("p h j -> p (h j)"), ident[:, :])
                    last.then_inc(pT_ps, 1)

            def weighted_values(p):
                pe.wait_ge(pT_ready, 2 * (p + 1))
                if p == 0:
                    pe.wait_ge(v_ready, 8)
                else:
                    pe.wait_ge(aT_ready, p)
                for a in range(2):
                    for q in range(2):
                        for r in range(4):
                            at = (2 * p + a) * 256 + 64 * r + 32 * q
                            m = 2 * r + q
                            last = mm(p6[32 * r:32 * r + 32, a * T:(a + 1) * T], vbd[:, at:at + 32],
                                      pT[:, p % 2, m * 128 + a * T:m * 128 + (a + 1) * T],
                                      start=(q == 0), stop=(q == 1), tile_position=(0, 32 * r))
                last.then_inc(o_ps, 1)

            def project(p):
                pe.wait_ge(aT_ready, p + 1)
                if p >= 1:
                    pe.wait_ge(x2_ready, p)
                mm(p7[:, 0:C], aT[:, p % 2, :], wout_sb[:, :], start=True, stop=True).then_inc(y_ps, 1)

            pe.wait_ge(c_pair, 2)
            pe.wait_ge(pen_ready, 2)
            pe.wait_ge(kbd_ready, 8)
            pe.wait_ge(ld_wout, 16)
            scores(0)
            for p in range(NP + 2):
                if p + 1 < NP:
                    scores(p + 1)
                if p >= 2:
                    weighted_values(p - 2)
                if 1 <= p <= NP:
                    transpose_probs(p - 1)
                if p >= 2:
                    project(p - 2)

            for n in range(NP):
                pe.wait_ge(xn2_ready, n + 1)
                last = nc.tensor.transpose(pT2[:, 128 * n:128 * n + 128], xn2[:, n, :], ident[:, :])
                if n % 4 == 3:
                    last.then_inc(x2T_ps, 1)
            pe.wait_ge(ld_router, 32)
            pe.wait_ge(x2_ready, NP)
            for n in range(NP):
                if n % 4 == 0:
                    pe.wait_ge(x2T_ready, n // 4 + 1)
                last = mm(p7[:, n * E:(n + 1) * E], xn2T[:, n * P:(n + 1) * P], rw_sb[:, :], start=True, stop=True)
            last.then_inc(lg_ps, 1)
            pe.wait_ge(oh_ready, 2)
            pe.wait_ge(c_route, 6)
            ohf = [oh[:, k, :, :].rearrange("p n e -> p (n e)") for k in range(2)]
            mm(p6[:, 0:NP * E], before[:, :], ohf[0], start=True, stop=True)
            mm(p6[:, NP * E:2 * NP * E], before[:, :], ohf[1], start=True, stop=False)
            mm(p6[:, NP * E:2 * NP * E], same[:, :], ohf[0], start=False, stop=True).then_inc(pos_ps, 1)
            pe.wait_ge(disp_ready, 2)
            for n in range(NP):
                if n >= 4:
                    pe.wait_ge(xe_ready, n - 3)
                mm(BANKS[n % 4][:, 0:PS], xn2[:, n, :], disp[:, n, :], start=True, stop=True).then_inc(xe_ps, 1)

            def up(m):
                e, c = divmod(m, FC)
                if m < 2:
                    pe.wait_ge(xe_ready, NP)
                else:
                    pe.wait_ge(u_ready, m - 1)
                if c == 0:
                    pe.wait_ge(ld_exp[e], 48)
                rhs = xe[:, e, :, :].rearrange("c n s -> c (n s)")
                mm(pS[m % 2][:, 0:ES], wfc_sb[:, e, 128 * c:128 * c + 128], rhs, start=True, stop=True)
                mm(pS[m % 2][:, 512:512 + ES], wg_sb[:, e, 128 * c:128 * c + 128], rhs,
                   start=True, stop=True).then_inc(hg_ps, 1)

            def down(m):
                e, c = divmod(m, FC)
                pe.wait_ge(z_ready, m + 1)
                if c == 0 and e >= 1:
                    pe.wait_ge(oT_ready, e)
                last = mm(pT2[:, 0:ES], wp_sb[:, e, c, :], z[:, m % 3, :], start=(c == 0), stop=(c == FC - 1))
                if c == FC - 1:
                    last.then_inc(f_ps, 1)

            def turn_coll(i):
                gr, h = divmod(i, 2)
                e0, ne = GROUPS[gr]
                w = ne * SLOTS
                if i >= 1:
                    pe.wait_ge(collT_ready, i)
                for j in range(4):
                    last = nc.tensor.transpose(pT2[0:w, 512 + 128 * j:512 + 128 * j + 128],
                                               coll[:, 4 * h + j, e0 * SLOTS:e0 * SLOTS + w], ident[:, :])
                last.then_inc(cT2_ps, 1)

            def turn_out(i):
                gr, h = divmod(i, 2)
                e0, ne = GROUPS[gr]
                w = ne * SLOTS
                pe.wait_ge(collT_ready, 6)
                if i >= 1:
                    pe.wait_ge(os_ready, i)
                pe.wait_ge(oT_ready, e0 + ne)
                for j in range(4):
                    last = nc.tensor.transpose(pT2[0:w, 512 + 128 * j:512 + 128 * j + 128],
                                               oT[:, gr, 4 * h + j, 0:w], ident[:, :])
                last.then_inc(os_ps, 1)

            def collect(i):
                gr, h = divmod(i, 2)
                w = GROUPS[gr][1] * SLOTS
                pe.wait_ge(os_ready, i + 1)
                for j in range(4):
                    last = mm((p6, p7)[h][:, 128 * j:128 * j + 128], collT[0:w, gr, 4 * h + j, :],
                              osl[0:w, i % 2, j, :], start=(gr == 0 and j == 0), stop=(gr == 2),
                              skip_group_check=True)
                last.then_inc(yf_ps, 1)

            M = E * FC
            extra = {6: lambda: (pe.wait_ge(coll_ready, 2), turn_coll(0)), 7: lambda: turn_coll(1),
                     8: lambda: turn_coll(2), 9: lambda: turn_coll(3), 10: lambda: turn_coll(4),
                     11: lambda: turn_coll(5),
                     15: lambda: turn_out(0), 17: lambda: (collect(0), turn_out(1)), 19: lambda: collect(1),
                     27: lambda: turn_out(2), 28: lambda: (collect(2), turn_out(3)), 29: lambda: collect(3)}
            for m in range(M + 2):
                if m < M:
                    up(m)
                if m >= 2:
                    down(m - 2)
                if m in extra:
                    extra[m]()
            turn_out(4)
            turn_out(5)
            collect(4)
            collect(5)

        @block.scalar
        def _(act):
            sc = nc.scalar
            for h in range(2):
                act.dma_start(c_sb[:, h * XH:(h + 1) * XH, :], c_v[:, h * XH:(h + 1) * XH, :]).then_inc(ld_ctx, 16)
            act.dma_start(wkv_sb[:, :], wkv).then_inc(ld_wkv, 16)
            for a in range(2):
                act.dma_start(mask_nat[64 * a:64 * a + 64, :, :],
                              mask.rearrange("(o n a) j -> o a n j", a=2, o=1)[:, a].broadcast_to([64, NP, T])
                              ).then_inc(ld_mask, 16)
                act.dma_start(mask_u8[32 * a:32 * a + 1, :, :],
                              mask.rearrange("(o n a) j -> o a n j", a=2, o=1)[:, a]).then_inc(ld_mask, 16)
            for h in range(2):
                act.wait_ge(cT_ps, h + 1)
                sc.activation(cT[:, 512 * h:512 * h + 512], pT2[:, 512 * h:512 * h + 512], ACT.Copy
                              ).then_inc(cT_ready, 1)
            act.wait_ge(bT_ps, 1)
            sc.activation(bT[:, :], p6[:, 0:77], ACT.Copy).then_inc(bT_ready, 1)
            act.wait_ge(bT_ready, 1)
            for f in range(2):
                act.wait_ge(k_ps, f + 1)
                sc.activation(ks[:, 512 * f:512 * f + 512], BANKS[2 + f], ACT.Identity,
                              bias=bk_sb[:, f:f + 1]).then_inc(k_ready, 1)
            act.wait_ge(c_head, 1)
            act.wait_ge(k_ready, 2)
            for h in range(4, 6):
                sc.activation(kbd[:, h, :], ks[:, :], ACT.Copy, scale=hmask[:, h:h + 1]).then_inc(kbd_ready, 1)
            act.wait_ge(c_zero, 1)
            for t in range(2):
                act.wait_ge(v_ps, t + 1)
                src = (p6, p7)[t][:, :].rearrange("p (x q d) -> p x q d", q=2, d=D)
                dst = vbd[:, 2048 * t:2048 * t + 2048].rearrange("p (x w) -> p x w", w=64)
                for s in range(2):
                    for q in range(2):
                        at = 48 * q + 8 * s
                        sc.activation(dst[64 * s:64 * s + 64, :, at:at + 8], src[64 * s:64 * s + 64, :, q, :],
                                      ACT.Copy).then_inc(v_ready, 1)
            act.wait_ge(ld_gate, 48)
            sc.activation(tgx[:, :], gx[:, :], ACT.Tanh).then_inc(tg_ready, 1)
            sc.activation(tgf[:, :], gf[:, :], ACT.Tanh).then_inc(tg_ready, 1)

            def exps(p):
                act.wait_ge(shifted, p + 1)
                sc.activation(pm[:, p % 2, :, :], pm[:, p % 2, :, :], ACT.Exp).then_inc(exped, 1)

            def attention_out(p):
                act.wait_ge(o_ps, p + 1)
                if p >= 2:
                    act.wait_ge(y_ps, p - 1)
                sc.activation(aT[:, p % 2, :], p6[:, 0:P], ACT.Identity, bias=bv_sb[:, 0:1]).then_inc(aT_ready, 1)

            def probs_out(p):
                if p >= 2:
                    act.wait_ge(o_ps, p - 1)
                for h in range(2):
                    act.wait_ge(pT_ps, 2 * p + h + 1)
                    sc.activation(pT[:, p % 2, 512 * h:512 * h + 512], pT2[:, 512 * h:512 * h + 512],
                                  ACT.Copy).then_inc(pT_ready, 1)

            for p in range(NP + 2):
                if p < NP:
                    exps(p)
                if p >= 2:
                    attention_out(p - 2)
                if 1 <= p <= NP:
                    probs_out(p - 1)
            for h in range(2):
                act.wait_ge(x2T_ps, h + 1)
                sc.activation(xn2T[:, 512 * h:512 * h + 512], pT2[:, 512 * h:512 * h + 512], ACT.Copy
                              ).then_inc(x2T_ready, 1)
            act.wait_ge(dl_ready, 1)
            sc.activation(ex[:, :], dl[:, :], ACT.Exp).then_inc(ex_ready, 1)
            for n in range(NP):
                act.wait_ge(xe_ps, n + 1)
                sc.activation(xe[:, :, n, :], BANKS[n % 4][:, 0:PS].rearrange("c (e s) -> c e s", e=E),
                              ACT.Copy).then_inc(xe_ready, 1)

            def hidden(m):
                e, c = divmod(m, FC)
                act.wait_ge(hg_ps, m + 1)
                if m >= 2:
                    act.wait_ge(u_ready, m - 1)
                sc.activation(hs[:, m % 2, :], pS[m % 2][:, 0:ES], ACT.Identity,
                              bias=bfc_sb[:, e, c:c + 1]).then_inc(h_ready, 1)

            def silu(m):
                act.wait_ge(u_ready, m + 1)
                sc.activation(z[:, m % 3, :], hg[:, m % 2, :], ACT.Silu).then_inc(z_ready, 1)

            def expert_out(e):
                gr = min(e // 3, 2)
                k = e - GROUPS[gr][0]
                act.wait_ge(f_ps, e + 1)
                sc.activation(oT[:, gr, :, k * SLOTS:(k + 1) * SLOTS],
                              pT2[:, 0:ES].rearrange("c (n s) -> c n s", n=NP), ACT.Identity,
                              bias=bp_sb[:, e:e + 1]).then_inc(oT_ready, 1)

            M = E * FC
            for m in range(M + 3):
                if m < M:
                    hidden(m)
                if 1 <= m <= M:
                    silu(m - 1)
                if m >= FC + 1 and (m - FC - 1) % FC == 1:
                    expert_out((m - FC - 1) // FC)

        @block.vector
        def _(dve):
            v = nc.vector
            n = [0]

            def then(ins):
                link(dve, dve_chain, n, ins)

            def norm_stats(src, st, m_v, k):
                then(v.bn_stats(st[:, k, :], src[:, k, :]))
                return v.bn_aggr(m_v[:, k, :], st[:, k, :])

            for h in range(2):
                dve.wait_ge(ld_x, 32)
                for k in range(h * XH, (h + 1) * XH):
                    v.bn_stats(stats[:, k, :], x_sb[:, k, :]).then_inc(dve_chain, 1)
                n[0] += XH
                dve.wait_ge(dve_chain, n[0])
                for k in range(h * XH, (h + 1) * XH):
                    last = v.bn_aggr(mv[:, k, :], stats[:, k, :])
                    if k < (h + 1) * XH - 1:
                        last.then_inc(dve_chain, 1)
                        n[0] += 1
                last.then_inc(var_ready, 1)
            for h in range(2):
                dve.wait_ge(rstd_ready, h + 1)
                for k in range(h * XH, (h + 1) * XH):
                    last = v.tensor_scalar(xn[:, k, :], x_sb[:, k, :], mv[:, k, 0:1], rstd[:, k:k + 1],
                                           ALU.subtract, ALU.mult)
                last.then_inc(xn_ready, 1)
            then(v.memset(penalty[:, :, :], 0.0))
            dve.wait_ge(ld_mask, 64)
            for a in range(2):
                v.tensor_scalar(penalty[32 * a:32 * a + 1, :, :], mask_u8[32 * a:32 * a + 1, :, :], MASKED, None,
                                ALU.mult).then_inc(pen_ready, 1)
            then(v.tensor_reduce(nmask[:, :], mask_nat[:, :, :], AX_X, ALU.add))
            then(v.tensor_scalar(live[:, :], nmask[:, :], -1.0, float(T), ALU.mult, ALU.add))
            then(v.reciprocal(rlive[:, :], live[:, :]))
            then(v.tensor_tensor(nmask[:, :], live[:, :], rlive[:, :], ALU.mult))
            then(v.tensor_tensor(live[:, :], nmask[:, :], nmask[:, :], ALU.subtract))
            then(v.tensor_scalar(nanfix[:, :], live[:, :], 1.0, None, ALU.add))
            for h in range(2):
                dve.wait_ge(xT_ps, h + 1)
                v.tensor_copy(xnT[:, 512 * h:512 * h + 512], pT2[:, 512 * h:512 * h + 512]).then_inc(xT_ready, 1)
            dve.wait_ge(c_head, 1)
            dve.wait_ge(k_ready, 2)
            for h in range(0, 4):
                v.tensor_scalar(kbd[:, h, :], ks[:, :], hmask[:, h:h + 1], None, ALU.mult).then_inc(kbd_ready, 1)
            dve.wait_ge(bT_ready, 1)
            for f in range(2):
                dve.wait_ge(q_ps, f + 1)
                v.tensor_scalar(qs[:, f, :], BANKS[f], bq_sb[:, f:f + 1], SCALE, ALU.add, ALU.mult
                                ).then_inc(q_ready, 1)

            def shift(p):
                dve.wait_ge(s_ps, p + 1)
                sv = pS[p % 2][:, :].rearrange("p (h j) -> p h j", h=H)
                then(v.tensor_reduce(negmax[:, p, :], sv, AX_X, ALU.max, negate=True))
                if p >= 2:
                    dve.wait_ge(normed, p - 1)
                v.tensor_tensor(pm[:, p % 2, :, :], sv, negmax[:, p, :].unsqueeze(2).broadcast_to([P, H, T]),
                                ALU.add).then_inc(shifted, 1)

            def sums(p):
                dve.wait_ge(exped, p + 1)
                then(v.tensor_reduce(ssum[:, p, :], pm[:, p % 2, :, :], AX_X, ALU.add))
                then(v.reciprocal(rsum[:, p, :], ssum[:, p, :]))
                v.tensor_scalar(rsn[:, p, :], rsum[:, p, :], nanfix[:, p:p + 1], None, ALU.mult
                                ).then_inc(rs_ready, 1)

            def residual(p):
                if p == 0:
                    dve.wait_ge(xb_ready, 1)
                    dve.wait_ge(tg_ready, 2)
                dve.wait_ge(y_ps, p + 1)
                v.scalar_tensor_tensor(out=x2[:, p, :], in0=p7[:, 0:C], scalar=tgx[:, 0:1], in1=xb[:, p, :],
                                       op0=ALU.mult, op1=ALU.add).then_inc(x2_ready, 1)
                dve.wait_ge(x2_ready, p + 1)
                last = norm_stats(x2, stats2, mv2, p)
                if p == NP - 1:
                    last.then_inc(var2_ready, 1)
                else:
                    then(last)

            for p in range(NP + 2):
                if p < NP:
                    shift(p)
                if 1 <= p <= NP:
                    sums(p - 1)
                if p >= 2:
                    residual(p - 2)
            dve.wait_ge(rstd2_ready, 1)
            for k in range(NP):
                v.tensor_scalar(xn2[:, k, :], x2[:, k, :], mv2[:, k, 0:1], rstd2[:, k:k + 1],
                                ALU.subtract, ALU.mult).then_inc(xn2_ready, 1)
            dve.wait_ge(lg_ps, 1)
            dve.wait_ge(c_route, 6)
            then(v.tensor_tensor(lg[:, :, :], p7[:, 0:NP * E].rearrange("p (n e) -> p n e", n=NP),
                                 rb_bc[:, :].unsqueeze(1).broadcast_to([P, NP, E]), ALU.add))
            for k in range(NP):
                v.max(mx[:, k, :], lg[:, k, :]).then_inc(dve_chain, 1)
            n[0] += NP
            dve.wait_ge(dve_chain, n[0])
            for k in range(NP):
                v.max_index(ix[:, k, :], mx[:, k, :], lg[:, k, :]).then_inc(dve_chain, 1)
            n[0] += NP
            dve.wait_ge(dve_chain, n[0])
            then(v.tensor_copy(idf[:, :, :].rearrange("p k n -> p n k"), ix[:, :, 0:2]))
            for k in range(2):
                v.tensor_tensor(oh[:, k, :, :], iota_e[:, :].unsqueeze(1).broadcast_to([P, NP, E]),
                                idf[:, k, :].unsqueeze(2).broadcast_to([P, NP, E]), ALU.is_equal
                                ).then_inc(oh_ready, 1)
            v.tensor_tensor(dl[:, :], mx[:, :, 1], mx[:, :, 0], ALU.subtract).then_inc(dl_ready, 1)
            dve.wait_ge(pos_ps, 1)
            dve.wait_ge(oh_ready, 2)
            cnt = [p6[:, k * NP * E:(k + 1) * NP * E].rearrange("p (n e) -> p n e", n=NP) for k in range(2)]
            v.scalar_tensor_tensor(out=pos0[:, :, :].rearrange("p n e -> p (n e)"), in0=p6[:, 0:NP * E], scalar=1.0,
                                   in1=oh[:, 0, :, :].rearrange("p n e -> p (n e)"),
                                   op0=ALU.add, op1=ALU.mult).then_inc(dve_chain, 1)
            v.scalar_tensor_tensor(out=pos1[:, :, :].rearrange("p n e -> p (n e)"), in0=p6[:, NP * E:2 * NP * E],
                                   scalar=1.0, in1=oh[:, 1, :, :].rearrange("p n e -> p (n e)"),
                                   op0=ALU.add, op1=ALU.mult).then_inc(dve_chain, 1)
            n[0] += 2
            dve.wait_ge(dve_chain, n[0])
            then(v.tensor_tensor(slot[:, :, :], pos0[:, :, :], pos1[:, :, :], ALU.add))
            for a in range(2):
                q = slice(64 * a, 64 * a + 64)
                dvw = disp[q, :, :].rearrange("p n (e a s) -> p (n e) a s", a=2, s=CAP)[:, :, a, :]
                v.tensor_tensor(dvw, slot[q, :, :].rearrange("p n e -> p (n e)").unsqueeze(2)
                                .broadcast_to([T, NP * E, CAP]),
                                iota_s[q, :].unsqueeze(1).broadcast_to([T, NP * E, CAP]), ALU.is_equal
                                ).then_inc(disp_ready, 1)
            dve.wait_ge(ex_ready, 1)
            then(v.tensor_scalar(den[:, :], ex[:, :], 1.0, None, ALU.add))
            then(v.reciprocal(pr[:, 0, :], den[:, :]))
            then(v.tensor_tensor(pr[:, 1, :], ex[:, :], pr[:, 0, :], ALU.mult))
            for k, w in ((0, pw0), (1, pw1)):
                then(v.tensor_tensor(w[:, :, :], oh[:, k, :, :],
                                     pr[:, k, :].unsqueeze(2).broadcast_to([P, NP, E]), ALU.mult))
            then(v.tensor_tensor(pw[:, :, :], pw0[:, :, :], pw1[:, :, :], ALU.add))
            then(v.tensor_scalar(slotc[:, :, :], slot[:, :, :], float(CAP), None, ALU.min))
            dve.wait_ge(c_zero, 2)
            for a in range(2):
                q = slice(64 * a, 64 * a + 64)
                cv = coll[q, :, :].rearrange("p n (e a s) -> p (n e) a s", a=2, s=CAP)[:, :, a, :]
                v.tensor_tensor(cv, slotc[q, :, :].rearrange("p n e -> p (n e)").unsqueeze(2)
                                .broadcast_to([T, NP * E, CAP]),
                                iota_s[q, :].unsqueeze(1).broadcast_to([T, NP * E, CAP]), ALU.is_equal
                                ).then_inc(slot_ready, 1)

            def gate(m):
                e, c = divmod(m, FC)
                dve.wait_ge(h_ready, m + 1)
                if m >= 2:
                    dve.wait_ge(z_ready, m - 1)
                v.scalar_tensor_tensor(out=hg[:, m % 2, :], in0=pS[m % 2][:, 512:512 + ES],
                                       scalar=bg_sb[:, e, c:c + 1], in1=hs[:, m % 2, :],
                                       op0=ALU.add, op1=ALU.mult).then_inc(u_ready, 1)

            def coll_out(i):
                gr, h = divmod(i, 2)
                w = GROUPS[gr][1] * SLOTS
                dve.wait_ge(cT2_ps, i + 1)
                v.tensor_copy(collT[0:w, gr, 4 * h:4 * h + 4, :].rearrange("s n t -> s (n t)"),
                              pT2[0:w, 512:1024]).then_inc(collT_ready, 1)

            def slots_out(i):
                gr, h = divmod(i, 2)
                w = GROUPS[gr][1] * SLOTS
                dve.wait_ge(os_ps, i + 1)
                if i >= 2:
                    dve.wait_ge(yf_ps, i - 1)
                v.tensor_copy(osl[0:w, i % 2, :, :].rearrange("s n c -> s (n c)"),
                              pT2[0:w, 512:1024]).then_inc(os_ready, 1)

            M = E * FC
            after = {6: ("c", 0), 7: ("c", 1), 8: ("c", 2), 9: ("c", 3), 10: ("c", 4), 11: ("c", 5),
                     15: ("o", 0), 17: ("o", 1), 27: ("o", 2), 28: ("o", 3)}
            for m in range(M):
                gate(m)
                if m in after:
                    kind, i = after[m]
                    (coll_out if kind == "c" else slots_out)(i)
            slots_out(4)
            slots_out(5)
            for h in range(2):
                dve.wait_ge(yf_ps, 5 + h)
                v.scalar_tensor_tensor(out=fin[:, 4 * h:4 * h + 4, :].rearrange("p n c -> p (n c)"),
                                       in0=(p6, p7)[h][:, :], scalar=tgf[:, 0:1],
                                       in1=x2[:, 4 * h:4 * h + 4, :].rearrange("p n c -> p (n c)"),
                                       op0=ALU.mult, op1=ALU.add).then_inc(fin_ready, 1)


_INS = ["x", "ctx_1024", "mask_BxS2_bf0", "g_xattn", "g_ffn", "L0_xattn_Wq", "L0_xattn_bq", "L0_xattn_Wkv",
        "L0_xattn_bkv", "L0_xattn_Wout", "L0_xattn_bout", "L0_ffn_router_w", "L0_ffn_router_b",
        "L0_ffn_w_c_fc", "L0_ffn_b_c_fc", "L0_ffn_w_gate", "L0_ffn_b_gate", "L0_ffn_w_c_proj",
        "L0_ffn_b_c_proj"]
_OUTS = [((16, 64, 128), "float32")]


def kernel(**inputs):
    import numpy as _np
    import concourse.bacc as _bacc
    from concourse import mybir as _mybir
    from concourse.bass_utils import run_bass_kernel_spmd as _run

    nc = _bacc.Bacc("TRN2", target_bir_lowering=False, num_devices=1)
    arrays, args = {}, []
    for name in _INS:
        a = _np.ascontiguousarray(inputs[name])
        arrays[f"in_{name}_dram"] = a
        args.append(nc.dram_tensor(f"in_{name}_dram", a.shape, _mybir.dt.from_np(a.dtype), kind="ExternalInput").ap())
    for i, (shape, dtype) in enumerate(_OUTS):
        dt = _mybir.dt.from_np(_np.dtype(dtype))
        args.append(nc.dram_tensor(f"out_{i}_dram", shape, dt, kind="ExternalOutput").ap())
    gated_attention_moe(nc, *args)
    r = _run(nc, [arrays], core_ids=[0])
    got = tuple(r.results[0][f"out_{i}_dram"] for i in range(len(_OUTS)))
    return got[0]
```

```python
from contextlib import ExitStack

import concourse.bass as bass
from concourse import mybir

F32 = mybir.dt.float32
BF16 = mybir.dt.bfloat16
U8 = mybir.dt.uint8
U32 = mybir.dt.uint32
ALU = mybir.AluOpType
ACT = mybir.ActivationFunctionType
AX_X = mybir.AxisListType.X

EPS = 1e-5
MASKED = -1.0e30
LOAD_FACTOR = 1.2
TOP_K = 2


def gated_attention_moe(nc, x, ctx_in, mask, g_xattn, g_ffn, wq, bq, wkv, bkv, wout, bout,
                        router_w, router_b, w_fc, b_fc, w_gate, b_gate, w_proj, b_proj, out):
    B, T, C = x.shape
    E = router_w.shape[1]
    F = w_fc.shape[2]
    H = 16
    D = C // H
    CAP = int(LOAD_FACTOR * TOP_K * T // E)
    P = 2 * T
    NP = B // 2
    HALF = C // 2
    HH = H // 2
    FC = F // 128
    SLOTS = 2 * CAP
    PS = E * SLOTS
    ES = B * CAP
    GROUPS = [(0, 3), (3, 3), (6, 2)]
    GW = 3 * SLOTS
    SCALE = float(D) ** -0.5
    assert P == 128 and C == 128 and D == 8 and NP == 8 and E == 8

    with ExitStack() as stack:
        def sb(name, shape, dt=F32):
            return stack.enter_context(nc.sbuf_tensor(name, shape, dt))

        def ps(name, shape):
            return stack.enter_context(nc.psum_tensor(name, shape, F32))

        def sem(name):
            return stack.enter_context(nc.semaphore(name))

        x_sb = sb("x_sb", [P, NP, C])
        c_sb = sb("c_sb", [P, NP, C])
        xn = sb("xn", [P, NP, C])
        xnT = sb("xnT", [C, NP * P])
        cT = sb("cT", [C, NP * P])
        wq_sb = sb("wq_sb", [C, C])
        wkv_sb = sb("wkv_sb", [C, 2 * C])
        wout_sb = sb("wout_sb", [C, C])
        b_rows = sb("b_rows", [77, 128])
        bT = sb("bT", [128, 77])
        bq_sb, bk_sb, bv_sb = bT[:, 72:74], bT[:, 74:76], bT[:, 76:77]
        bout_bc = sb("bout_bc", [P, C])
        bqs = sb("bqs", [P, 2])
        gx = sb("gx", [P, 1])
        gf = sb("gf", [P, 1])
        tgx = sb("tgx", [P, 1])
        tgf = sb("tgf", [P, 1])
        warm = sb("warm", [P, 1])
        rw_sb = sb("rw_sb", [C, E])
        rb_bc = sb("rb_bc", [P, E])
        mask_nat = sb("mask_nat", [P, NP, T], U8)
        mask_u8 = sb("mask_u8", [64, NP, T], U8)
        penalty = sb("penalty", [64, NP, T], BF16)
        batch_row = sb("batch_row", [64, P], BF16)
        nmask = sb("nmask", [P, NP])
        live = sb("live", [P, NP])
        rlive = sb("rlive", [P, NP])
        nanfix = sb("nanfix", [P, NP])
        xt = sb("xt", [P, NP, C])
        wfc_sb = sb("wfc_sb", [C, E, F])
        wg_sb = sb("wg_sb", [C, E, F])
        wp_sb = sb("wp_sb", [128, E, FC, C])
        bfc_sb = bT[:, 0:E * FC].rearrange("p (e c) -> p e c", e=E)
        bg_sb = bT[:, E * FC:2 * E * FC].rearrange("p (e c) -> p e c", e=E)
        bp_sb = bT[:, 2 * E * FC:2 * E * FC + E]
        ident = sb("ident", [128, 128])
        hmask = sb("hmask", [P, HH])
        before = sb("before", [P, P], BF16)
        same = sb("same", [P, P], BF16)
        iota_e = sb("iota_e", [P, E])
        iota_s = sb("iota_s", [P, CAP])
        mhalf = sb("mhalf", [P, NP])
        stats = sb("stats", [P, NP, 6])
        mv = sb("mv", [P, NP, 2])
        veps = sb("veps", [P, NP])
        rstd = sb("rstd", [P, NP])
        stats2 = sb("stats2", [P, NP, 6])
        mv2 = sb("mv2", [P, NP, 2])
        veps2 = sb("veps2", [P, NP])
        rstd2 = sb("rstd2", [P, NP])
        ks = sb("ks", [P, 2 * NP * T])
        kbd = sb("kbd", [P, HH, 2 * NP * T])
        qbd = sb("qbd", [P, 2, NP, 2, T])
        vbd = sb("vbd", [P, B * HH * 32])
        pm = sb("pm", [P, 2, H, T])
        negmax = sb("negmax", [P, NP, H])
        ones_q = sb("ones_q", [P, 2, 32])
        rden = sb("rden", [C, 2, P])
        bvm = sb("bvm", [C, P])
        bias_y = sb("bias_y", [P, C])
        pT = sb("pT", [P, 2, HH * P])
        aT = sb("aT", [C, 2, P])
        tb = sb("tb", [P, C])
        xb = sb("xb", [P, NP, C])
        x2 = sb("x2", [P, NP, C])
        xn2 = xn
        xn2T = xnT[:, :].rearrange("c (n t) -> c n t", n=NP)
        lg = sb("lg", [P, NP, E])
        mx = sb("mx", [P, NP, 8])
        ix = sb("ix", [P, NP, 8], U32)
        idf = sb("idf", [P, 2, NP])
        oh = sb("oh", [P, 2, NP, E], BF16)
        pos0 = sb("pos0", [P, NP, E])
        pos1 = sb("pos1", [P, NP, E])
        slot = sb("slot", [P, NP, E])
        slotc = sb("slotc", [P, NP, E])
        dl = sb("dl", [P, NP])
        ex = sb("ex", [P, NP])
        den = sb("den", [P, NP])
        pr = sb("pr", [P, 2, NP])
        pw0 = sb("pw0", [P, NP, E])
        pw1 = sb("pw1", [P, NP, E])
        pw = sb("pw", [P, NP, E])
        disp = sb("disp", [P, NP, PS])
        coll = sb("coll", [P, NP, PS])
        kflat = kbd[:, :, :].rearrange("p h x -> p (h x)")
        collT = kflat[:, 0:3 * NP * P].rearrange("p (g n t) -> p g n t", g=3, n=NP)
        oT = kflat[:, 3 * NP * P:3 * NP * (P + GW)].rearrange("p (g n w) -> p g n w", g=3, n=NP)
        xe = vbd[:, 0:E * NP * SLOTS].rearrange("p (e n s) -> p e n s", e=E, n=NP)
        hs = sb("hs", [128, 2, ES])
        hg = sb("hg", [128, 2, ES])
        z = sb("z", [128, 3, ES])
        osl = sb("osl", [128, 2, 4, C])
        fin = c_sb

        pS = [ps(f"pS{r}", [128, 1024]) for r in range(2)]
        pT2 = ps("pT2", [128, 1024])
        p6 = ps("p6", [128, 512])
        p7 = ps("p7", [128, 512])
        OS_PS = [pT2[:, 512:1024]] * 5 + [pS[0][:, 0:512]]
        LATE = 5
        BANKS = [pS[0][:, 0:512], pS[0][:, 512:1024], pS[1][:, 0:512], pS[1][:, 512:1024]]

        X2T_PS = [p6[:, 2 * P:3 * P]] * LATE + [BANKS[p % 2][:, 0:P] for p in range(LATE, NP)]
        LG_PS = [p7[:, C:C + E]] * LATE + [BANKS[2][:, 0:E]] * (NP - LATE)

        ld_x = [sem(f"ld_x{h}") for h in range(2)]
        ld_ctx = [sem(f"ld_ctx{h}") for h in range(2)]
        ld_wq = sem("ld_wq")
        ld_wkv = sem("ld_wkv")
        ld_bias = sem("ld_bias")
        ld_gate = sem("ld_gate")
        ld_mask = sem("ld_mask")
        ld_wout = sem("ld_wout")
        ld_router = sem("ld_router")
        bT_ps = sem("bT_ps")
        bT_ready = sem("bT_ready")
        ld_exp = [sem(f"ld_exp{e}") for e in range(E)]
        st_out = sem("st_out")
        pool_chain = sem("pool_chain")
        dve_chain = sem("dve_chain")
        c_ident = sem("c_ident")
        c_head = sem("c_head")
        c_pair = sem("c_pair")
        c_route = sem("c_route")
        c_zero = sem("c_zero")
        c_quarter = sem("c_quarter")
        pen_ready = sem("pen_ready")
        var_ready = sem("var_ready")
        rstd_ready = sem("rstd_ready")
        xn_ready = sem("xn_ready")
        cT_ps = sem("cT_ps")
        cT_ready = sem("cT_ready")
        xT_ps = sem("xT_ps")
        xT_ready = sem("xT_ready")
        k_ps = sem("k_ps")
        k_ready = sem("k_ready")
        q_ps = sem("q_ps")
        v_ps = sem("v_ps")
        v_ready = sem("v_ready")
        kbd_ready_act = sem("kbd_ready_act")
        kbd_ready_dve = sem("kbd_ready_dve")
        kbd_ready_pool = sem("kbd_ready_pool")
        qbd_ready_act = sem("qbd_ready_act")
        qbd_ready_dve = sem("qbd_ready_dve")
        qbd_zero = sem("qbd_zero")
        bqs_ready = sem("bqs_ready")
        s_ps = sem("s_ps")
        shifted = sem("shifted")
        exped = sem("exped")
        bvm_ready = sem("bvm_ready")
        bvy_ps = sem("bvy_ps")
        bias_y_ready = sem("bias_y_ready")
        nan_ready = sem("nan_ready")
        lg_read = sem("lg_read")
        x2_stats = sem("x2_stats")
        disp_zero = sem("disp_zero")
        xe_ready_act = sem("xe_ready_act")
        xe_ready_dve = sem("xe_ready_dve")
        pT_ps = sem("pT_ps")
        pT_ready = sem("pT_ready")
        o_ps = sem("o_ps")
        aT_ready = sem("aT_ready")
        y_ps = sem("y_ps")
        x2_ready = sem("x2_ready")
        xb_ready = sem("xb_ready")
        tg_ready = sem("tg_ready")
        xn2_ready = sem("xn2_ready")
        rstd2_late = sem("rstd2_late")
        xn2_late = sem("xn2_late")
        x2T_ps = sem("x2T_ps")
        x2T_ready = sem("x2T_ready")
        lg_ps = sem("lg_ps")
        oh_ready = sem("oh_ready")
        pos_ps = sem("pos_ps")
        dl_ready = sem("dl_ready")
        ex_ready = sem("ex_ready")
        disp_ready = sem("disp_ready")
        slot_ready = sem("slot_ready")
        coll_ready = sem("coll_ready")
        xe_ps = sem("xe_ps")
        hg_ps = sem("hg_ps")
        h_ready = sem("h_ready")
        u_ready = sem("u_ready")
        z_ready = sem("z_ready")
        f_ps = sem("f_ps")
        oT_ready = sem("oT_ready")
        cT2_ps = sem("cT2_ps")
        collT_ready = sem("collT_ready")
        os_ps = sem("os_ps")
        os_ready = sem("os_ready")
        yf_ps = sem("yf_ps")
        fin_ready = sem("fin_ready")

        x_v = x.rearrange("(n a) i c -> (a i) n c", a=2)
        c_v = ctx_in.rearrange("(n a) i c -> (a i) n c", a=2)
        out_v = out.rearrange("(n a) i c -> (a i) n c", a=2)
        XH = NP // 2

        ks_v = ks[:, :].rearrange("p (f g x) -> p f g x", f=2, g=2)
        kbd_v = kbd[:, :, :].rearrange("p h (f g x) -> p h f g x", f=2, g=2)

        def row(v):
            return v.rearrange("(o c) -> o c", o=1)

        def link(eng, chain, count, ins):
            count[0] += 1
            ins.then_inc(chain, 1)
            eng.wait_ge(chain, count[0])

        block = stack.enter_context(nc.Block())

        @block.sync
        def _(sp):
            for h in range(2):
                sp.dma_start(x_sb[:, h * XH:(h + 1) * XH, :], x_v[:, h * XH:(h + 1) * XH, :]).then_inc(ld_x[h], 16)
            sp.dma_start(b_rows[0:32, :], b_fc.rearrange("e o (c p) -> (e o c) p", p=128)).then_inc(ld_bias, 16)
            sp.dma_start(b_rows[32:64, :], b_gate.rearrange("e o (c p) -> (e o c) p", p=128)).then_inc(ld_bias, 16)
            sp.dma_start(b_rows[64:72, :], b_proj.rearrange("e o c -> (e o) c")).then_inc(ld_bias, 16)
            for at, vec in ((72, bq), (74, bkv[0:C])):
                sp.dma_start(b_rows[at:at + 2, :].rearrange("f (a r) -> f a r", a=2),
                             vec.rearrange("(f a r) -> f a r", f=2, a=1).broadcast_to([2, 2, HALF])
                             ).then_inc(ld_bias, 16)
            sp.dma_start(b_rows[76:77, :], row(bkv[C:2 * C])).then_inc(ld_bias, 16)
            for a in range(2):
                sp.dma_start(mask_nat[64 * a:64 * a + 64, :, :],
                              mask.rearrange("(o n a) j -> o a n j", a=2, o=1)[:, a].broadcast_to([64, NP, T])
                              ).then_inc(ld_mask, 16)
                sp.dma_start(mask_u8[32 * a:32 * a + 1, :, :],
                              mask.rearrange("(o n a) j -> o a n j", a=2, o=1)[:, a]).then_inc(ld_mask, 16)
            sp.dma_start(wout_sb[:, :], wout).then_inc(ld_wout, 16)
            sp.dma_start(bout_bc[:, :], row(bout).broadcast_to([P, C])).then_inc(ld_gate, 16)
            sp.dma_start(gx[:, :], row(g_xattn).broadcast_to([P, 1])).then_inc(ld_gate, 16)
            sp.dma_start(gf[:, :], row(g_ffn).broadcast_to([P, 1])).then_inc(ld_gate, 16)
            sp.dma_start(rw_sb[:, :], router_w).then_inc(ld_router, 16)
            sp.dma_start(rb_bc[:, :], row(router_b).broadcast_to([P, E])).then_inc(ld_router, 16)
            for e in range(E):
                sp.dma_start(wfc_sb[:, e, :], w_fc[e]).then_inc(ld_exp[e], 16)
                sp.dma_start(wg_sb[:, e, :], w_gate[e]).then_inc(ld_exp[e], 16)
                sp.dma_start(wp_sb[:, e, :, :], w_proj[e].rearrange("(c p) o -> p c o", p=128)).then_inc(ld_exp[e], 16)
            for h in range(2):
                sp.wait_ge(fin_ready, h + 1)
                sp.dma_start(out_v[:, h * XH:(h + 1) * XH, :], fin[:, h * XH:(h + 1) * XH, :]).then_inc(st_out, 16)
            sp.wait_ge(st_out, 32)

        @block.gpsimd
        def _(pool):
            n = [0]
            g = nc.gpsimd

            def then(ins):
                link(pool, pool_chain, n, ins)

            then(g.memset(ident[:, :], 0.0))
            g.affine_select(out=ident[:, :], in_=ident[:, :], compare_op=ALU.not_equal, fill=1.0, base=0,
                            pattern=[[-1, 128]], channel_multiplier=1).then_inc(c_ident, 1)
            then(g.memset(hmask[:, :], 1.0))
            for a in range(2):
                part = hmask[64 * a:64 * a + 64, :]
                then(g.affine_select(out=part, in_=part, compare_op=ALU.is_ge, fill=0.0, base=0,
                                     pattern=[[-D, HH]], channel_multiplier=1))
                then(g.affine_select(out=part, in_=part, compare_op=ALU.is_ge, fill=0.0, base=D - 1,
                                     pattern=[[D, HH]], channel_multiplier=-1))
            g.memset(mhalf[:, :], -0.5).then_inc(c_head, 1)
            g.memset(vbd[:, 0:B * HH * 16], 0.0).then_inc(c_zero, 1)
            for h in range(2):
                lo, hi = h * XH, (h + 1) * XH
                pool.wait_ge(var_ready, h + 1)
                then(g.tensor_scalar(veps[:, lo:hi], mv[:, lo:hi, 1], EPS, None, ALU.add))
                g.tensor_tensor(rstd[:, lo:hi], veps[:, lo:hi], mhalf[:, lo:hi], ALU.pow).then_inc(rstd_ready, 1)
            g.memset(vbd[:, B * HH * 16:], 0.0).then_inc(c_zero, 1)
            then(g.memset(batch_row[:, :], 0.0))
            g.memset(batch_row[0:1, 0:T], 1.0).then_inc(c_pair, 1)
            pool.wait_ge(c_pair, 1)
            g.memset(batch_row[32:33, T:P], 1.0).then_inc(c_pair, 1)
            pool.wait_ge(c_pair, 2)
            then(g.memset(ones_q[:, :, :], 0.0))
            for i, (a, q) in enumerate(((0, 0), (0, 1), (1, 0), (1, 1))):
                at = 16 * q + 8 * a
                g.memset(ones_q[64 * a:64 * a + 64, q, at:at + 8], 1.0).then_inc(c_quarter, 1)
                pool.wait_ge(c_quarter, i + 1)
            pool.wait_ge(k_ready, 2)
            for h in range(0, 4):
                g.tensor_scalar(kbd_v[:, h, :, 1, :], ks_v[:, :, 1, :], hmask[:, h:h + 1], None, ALU.mult
                                ).then_inc(kbd_ready_pool, 1)
            pool.wait_ge(nan_ready, 1)
            then(g.tensor_tensor(xt[:, :, :], x_sb[:, :, :], nanfix[:, :].unsqueeze(2).broadcast_to([P, NP, C]),
                                 ALU.add))
            then(g.memset(before[:, :], 1.0))
            then(g.affine_select(out=before[:, :], in_=before[:, :], compare_op=ALU.is_gt, fill=0.0,
                                 base=0, pattern=[[1, P]], channel_multiplier=-1))
            g.memset(before[0:T, T:P], 0.0).then_inc(c_route, 1)
            pool.wait_ge(c_route, 1)
            then(g.memset(same[:, :], 1.0))
            g.memset(same[0:T, T:P], 0.0).then_inc(c_route, 1)
            pool.wait_ge(c_route, 2)
            g.memset(same[T:P, 0:T], 0.0).then_inc(c_route, 1)
            pool.wait_ge(c_route, 3)
            g.iota(iota_e[:, :], [[1, E]], base=0, channel_multiplier=0,
                   allow_small_or_imprecise_dtypes=True).then_inc(c_route, 1)
            g.iota(iota_s[:, :], [[1, CAP]], base=1, channel_multiplier=0,
                   allow_small_or_imprecise_dtypes=True).then_inc(c_route, 1)
            pool.wait_ge(bias_y_ready, 1)
            pool.wait_ge(tg_ready, 1)
            then(g.tensor_scalar(tb[:, :], bias_y[:, :], tgx[:, 0:1], None, ALU.mult))
            g.tensor_tensor(xb[:, :, :], xt[:, :, :], tb[:, :].unsqueeze(1).broadcast_to([P, NP, C]),
                            ALU.add).then_inc(xb_ready, 1)
            g.memset(disp[:, :, :], 0.0).then_inc(disp_zero, 1)
            g.memset(coll[:, :, :], 0.0).then_inc(disp_zero, 1)
            for p in range(NP):
                pool.wait_ge(x2_stats, p + 1)
                then(g.tensor_scalar(veps2[:, p:p + 1], mv2[:, p, 1:2], EPS, None, ALU.add))
                power = g.tensor_tensor(rstd2[:, p:p + 1], veps2[:, p:p + 1], mhalf[:, p:p + 1], ALU.pow)
                if p < LATE:
                    then(power)
                    g.tensor_scalar(xn2[:, p, :], x2[:, p, :], mv2[:, p, 0:1], rstd2[:, p:p + 1],
                                    ALU.subtract, ALU.mult).then_inc(xn2_ready, 1)
                else:
                    power.then_inc(rstd2_late, 1)
            for a in range(2):
                pool.wait_ge(slot_ready, a + 1)
                q = slice(64 * a, 64 * a + 64)
                cv = coll[q, :, :].rearrange("p n (e a s) -> p (n e) a s", a=2, s=CAP)[:, :, a, :]
                pv = pw[q, :, :].rearrange("p n e -> p (n e)").unsqueeze(2).broadcast_to([T, NP * E, CAP])
                g.tensor_tensor(cv, cv, pv, ALU.mult).then_inc(coll_ready, 1)
                pool.wait_ge(coll_ready, a + 1)

        @block.tensor
        def _(pe):
            mm = nc.tensor.matmul

            def keep_busy(bank, times):
                for _ in range(times):
                    mm(bank[:, 0:128], ident[:, :], ident[:, :], start=True, stop=True)

            pe.wait_ge(c_ident, 1)
            keep_busy(BANKS[1], 7)
            for h in range(2):
                pe.wait_ge(ld_ctx[h], 16)
                for j in range(XH):
                    last = nc.tensor.transpose(pT2[:, 512 * h + 128 * j:512 * h + 128 * j + 128],
                                               c_sb[:, h * XH + j, :], ident[:, :])
                last.then_inc(cT_ps, 1)
                keep_busy(BANKS[1], 2)
            pe.wait_ge(cT_ready, 2)
            pe.wait_ge(ld_wkv, 16)
            cTv = cT[:, :].rearrange("c (n a j) -> c a n j", a=2, j=T)
            for f in range(2):
                for a in range(2):
                    last = mm(BANKS[2 + f][64 * a:64 * a + 64, :], wkv_sb[:, HALF * f:HALF * f + HALF],
                              cTv[:, a], start=True, stop=True, tile_position=(0, 64 * a))
                last.then_inc(k_ps, 1)
            pe.wait_ge(ld_bias, 16 * 6)
            nc.tensor.transpose(BANKS[0][:, 0:77], b_rows[:, :], ident[0:77, 0:77]).then_inc(bT_ps, 1)
            for h in range(2):
                pe.wait_ge(xn_ready, h + 1)
                for j in range(XH):
                    last = nc.tensor.transpose(pT2[:, 512 * h + 128 * j:512 * h + 128 * j + 128],
                                               xn[:, h * XH + j, :], ident[:, :])
                last.then_inc(xT_ps, 1)
            keep_busy(BANKS[1], 2)
            pe.wait_ge(xT_ready, 2)
            pe.wait_ge(ld_wq, 16)
            xTv = xnT[:, :].rearrange("c (n a j) -> c a n j", a=2, j=T)
            for f in range(2):
                for a in range(2):
                    last = mm((p6, p7)[f][64 * a:64 * a + 64, :], wq_sb[:, HALF * f:HALF * f + HALF],
                              xTv[:, a], start=True, stop=True, tile_position=(0, 64 * a))
                last.then_inc(q_ps, 1)

            kv = kbd[:, :, :].rearrange("p h (f n j) -> p f n h j", f=2, n=NP)

            def scores(p):
                if p >= 2:
                    pe.wait_ge(shifted, p - 1)
                if p == NP // 2:
                    pe.wait_ge(qbd_ready_dve, 4)
                    pe.wait_ge(qbd_ready_act, 4)
                    pe.wait_ge(kbd_ready_act, 7)
                    pe.wait_ge(kbd_ready_pool, 4)
                for f in range(2):
                    bank = pS[p % 2][:, 512 * f:512 * f + 512]
                    mm(bank, batch_row[:, :], penalty[:, p, :].unsqueeze(1).broadcast_to([64, HH, T]),
                       start=True, stop=False)
                    last = mm(bank, qbd[:, f, p, :, :].rearrange("p a i -> p (a i)"), kv[:, f, p],
                              start=False, stop=True)
                last.then_inc(s_ps, 1)

            def transpose_probs(p):
                pe.wait_ge(exped, p + 1)
                for h in range(2):
                    if p == 0:
                        pe.wait_ge(v_ready, 8)
                    else:
                        pe.wait_ge(pT_ready, 2 * (p - 1) + h + 1)
                    for m in range(4 * h, 4 * h + 4):
                        last = nc.tensor.transpose(
                            pT2[:, 128 * m:128 * m + 128],
                            pm[:, p % 2, 2 * m:2 * m + 2, :].rearrange("p h j -> p (h j)"), ident[:, :])
                    last.then_inc(pT_ps, 1)

            def weighted_values(p):
                pe.wait_ge(pT_ready, 2 * (p + 1))
                if p == 0:
                    pe.wait_ge(qbd_ready_dve, 4)
                else:
                    pe.wait_ge(aT_ready, p)
                if p >= 3:
                    pe.wait_ge(x2T_ready, p - 2)
                for a in range(2):
                    for q in range(2):
                        for r in range(4):
                            at = (2 * p + a) * 256 + 64 * r + 32 * q
                            m = 2 * r + q
                            last = mm(p6[32 * r:32 * r + 32, a * T:(a + 1) * T], vbd[:, at:at + 32],
                                      pT[:, p % 2, m * 128 + a * T:m * 128 + (a + 1) * T],
                                      start=(q == 0), stop=(q == 1), tile_position=(0, 32 * r))
                for q in range(2):
                    for r in range(4):
                        m = 2 * r + q
                        last = mm(p6[32 * r:32 * r + 32, P:2 * P], ones_q[:, q, :],
                                  pT[:, p % 2, m * 128:m * 128 + 128],
                                  start=(q == 0), stop=(q == 1), tile_position=(0, 32 * r))
                last.then_inc(o_ps, 1)

            def turn_x2(p):
                if p < LATE:
                    pe.wait_ge(aT_ready, p + 3)
                    pe.wait_ge(xn2_ready, p + 1)
                else:
                    if p >= LATE + 2:
                        pe.wait_ge(x2T_ready, p - 1)
                    pe.wait_ge(xn2_late, p + 1 - LATE)
                nc.tensor.transpose(X2T_PS[p], xn2[:, p, :], ident[:, :]).then_inc(x2T_ps, 1)

            def logits(p):
                pe.wait_ge(x2T_ready, p + 1)
                if p < LATE:
                    pe.wait_ge(x2_ready, p + 3)
                if p >= 1:
                    pe.wait_ge(lg_read, p)
                mm(LG_PS[p], xn2T[:, p, :], rw_sb[:, :], start=True, stop=True).then_inc(lg_ps, 1)

            def project(p):
                pe.wait_ge(aT_ready, p + 1)
                if p >= 1:
                    pe.wait_ge(x2_ready, p)
                if p >= 3:
                    pe.wait_ge(lg_read, min(p - 2, LATE))
                mm(p7[:, 0:C], aT[:, p % 2, :], wout_sb[:, :], start=True, stop=True).then_inc(y_ps, 1)

            def values(t):
                for b in range(8 * t, 8 * t + 8):
                    for s in range(2):
                        last = mm(pT2[64 * s:64 * s + 64, b * 64:b * 64 + 64],
                                  cT[:, b * T:(b + 1) * T], wv[:, s], start=True, stop=True,
                                  tile_position=(0, 64 * s))
                last.then_inc(v_ps, 1)

            wv = wkv_sb[:, C:2 * C].rearrange("c (m s d) -> c s m d", s=2, d=D)
            values(0)
            pe.wait_ge(c_pair, 2)
            pe.wait_ge(pen_ready, 2)
            pe.wait_ge(bT_ready, 1)
            pe.wait_ge(qbd_ready_dve, 2)
            pe.wait_ge(qbd_ready_act, 2)
            pe.wait_ge(kbd_ready_act, 3)
            pe.wait_ge(kbd_ready_dve, 5)
            scores(0)
            values(1)
            scores(1)
            pe.wait_ge(qbd_ready_act, 4)
            pe.wait_ge(bvm_ready, 1)
            pe.wait_ge(ld_wout, 16)
            mm(p7[:, 0:C], bvm[:, :], wout_sb[:, :], start=True, stop=True).then_inc(bvy_ps, 1)
            pe.wait_ge(c_quarter, 4)
            pe.wait_ge(ld_router, 32)
            for p in range(NP + 3):
                if p >= 6:
                    logits(p - 6)
                if p >= NP - 1:
                    keep_busy(BANKS[1], 2)
                if 1 <= p < NP - 1:
                    scores(p + 1)
                if 1 <= p <= NP:
                    transpose_probs(p - 1)
                if p >= 3:
                    if p == 3:
                        pe.wait_ge(bias_y_ready, 1)
                    project(p - 3)
                if p >= 5:
                    if p == NP + 1:
                        keep_busy(BANKS[1], 2)
                    turn_x2(p - 5)
                if p >= NP:
                    keep_busy(BANKS[3], 2)
                if 2 <= p < NP + 2:
                    weighted_values(p - 2)
            for p in range(LATE, NP):
                keep_busy(BANKS[3], 2)
                if p < NP - 1:
                    turn_x2(p + 1)
                keep_busy(BANKS[3], 0)
                logits(p)
            keep_busy(BANKS[3], 0)
            pe.wait_ge(oh_ready, 2)
            pe.wait_ge(c_route, 5)
            ohf = [oh[:, k, :, :].rearrange("p n e -> p (n e)") for k in range(2)]
            mm(p6[:, 0:NP * E], before[:, :], ohf[0], start=True, stop=True)
            mm(p6[:, NP * E:2 * NP * E], before[:, :], ohf[1], start=True, stop=False)
            mm(p6[:, NP * E:2 * NP * E], same[:, :], ohf[0], start=False, stop=True).then_inc(pos_ps, 1)
            keep_busy(BANKS[3], 9)
            for n in range(NP):
                pe.wait_ge(disp_ready, 2 * (n // 4 + 1))
                if n >= 4:
                    pe.wait_ge((xe_ready_act, xe_ready_dve)[n % 2], n // 2 - 1)
                mm(BANKS[n % 4][:, 0:PS], xn2[:, n, :], disp[:, n, :], start=True, stop=True).then_inc(xe_ps, 1)

            def up(m):
                e, c = divmod(m, FC)
                if m < 2:
                    pe.wait_ge(xe_ready_act, NP // 2)
                    pe.wait_ge(xe_ready_dve, NP // 2)
                else:
                    pe.wait_ge(u_ready, m - 1)
                if c == 0:
                    pe.wait_ge(ld_exp[e], 48)
                rhs = xe[:, e, :, :].rearrange("c n s -> c (n s)")
                mm(pS[m % 2][:, 0:ES], wfc_sb[:, e, 128 * c:128 * c + 128], rhs, start=True, stop=True)
                mm(pS[m % 2][:, 512:512 + ES], wg_sb[:, e, 128 * c:128 * c + 128], rhs,
                   start=True, stop=True).then_inc(hg_ps, 1)

            def down(m):
                e, c = divmod(m, FC)
                pe.wait_ge(z_ready, m + 1)
                if c == 0 and e >= 1:
                    pe.wait_ge(oT_ready, e)
                last = mm(pT2[:, 0:ES], wp_sb[:, e, c, :], z[:, m % 3, :], start=(c == 0), stop=(c == FC - 1))
                if c == FC - 1:
                    last.then_inc(f_ps, 1)

            def turn_coll(i):
                gr, h = divmod(i, 2)
                e0, ne = GROUPS[gr]
                w = ne * SLOTS
                if i >= 1:
                    pe.wait_ge(collT_ready, i)
                for j in range(4):
                    last = nc.tensor.transpose(pT2[0:w, 512 + 128 * j:512 + 128 * j + 128],
                                               coll[:, 4 * h + j, e0 * SLOTS:e0 * SLOTS + w], ident[:, :])
                last.then_inc(cT2_ps, 1)

            def turn_out(i):
                gr, h = divmod(i, 2)
                e0, ne = GROUPS[gr]
                w = ne * SLOTS
                pe.wait_ge(collT_ready, 6)
                if 1 <= i < 5:
                    pe.wait_ge(os_ready, i)
                pe.wait_ge(oT_ready, e0 + ne)
                for j in range(4):
                    last = nc.tensor.transpose(OS_PS[i][0:w, 128 * j:128 * j + 128],
                                               oT[:, gr, 4 * h + j, 0:w], ident[:, :])
                last.then_inc(os_ps, 1)

            def collect(i):
                gr, h = divmod(i, 2)
                w = GROUPS[gr][1] * SLOTS
                pe.wait_ge(os_ready, i + 1)
                for j in range(4):
                    last = mm((p6, p7)[h][:, 128 * j:128 * j + 128], collT[0:w, gr, 4 * h + j, :],
                              osl[0:w, i % 2, j, :], start=(gr == 0 and j == 0), stop=(gr == 2),
                              skip_group_check=True)
                last.then_inc(yf_ps, 1)

            M = E * FC
            extra = {10: lambda: (pe.wait_ge(coll_ready, 2), turn_coll(0)), 11: lambda: turn_coll(1),
                     12: lambda: turn_coll(2), 13: lambda: turn_coll(3), 14: lambda: turn_coll(4),
                     15: lambda: turn_coll(5),
                     16: lambda: turn_out(0), 17: lambda: (collect(0), turn_out(1)), 19: lambda: collect(1),
                     27: lambda: turn_out(2), 28: lambda: (collect(2), turn_out(3)), 29: lambda: collect(3)}
            for m in range(M + 2):
                if m < M:
                    up(m)
                if m >= 2:
                    down(m - 2)
                if m in extra:
                    extra[m]()
            turn_out(4)
            pe.wait_ge(u_ready, E * FC)
            turn_out(5)
            collect(4)
            collect(5)

        @block.scalar
        def _(act):
            sc = nc.scalar
            for h in range(2):
                act.dma_start(c_sb[:, h * XH:(h + 1) * XH, :], c_v[:, h * XH:(h + 1) * XH, :]).then_inc(ld_ctx[h], 16)
            act.dma_start(wkv_sb[:, :], wkv).then_inc(ld_wkv, 16)
            act.dma_start(wq_sb[:, :], wq).then_inc(ld_wq, 16)
            act.wait_ge(c_ident, 1)
            sc.activation(warm[:, :], ident[:, 0:1], ACT.Exp)
            for h in range(2):
                act.wait_ge(cT_ps, h + 1)
                sc.activation(cT[:, 512 * h:512 * h + 512], pT2[:, 512 * h:512 * h + 512], ACT.Copy
                              ).then_inc(cT_ready, 1)
            act.wait_ge(bT_ps, 1)
            sc.activation(bT[:, :], BANKS[0][:, 0:77], ACT.Copy).then_inc(bT_ready, 1)
            act.wait_ge(bT_ready, 1)
            act.wait_ge(k_ps, 1)
            sc.activation(ks[:, 0:512], BANKS[2], ACT.Identity, bias=bk_sb[:, 0:1]).then_inc(k_ready, 1)
            act.wait_ge(xT_ps, 2)
            sc.activation(xnT[:, 512:1024], pT2[:, 512:1024], ACT.Copy).then_inc(xT_ready, 1)
            act.wait_ge(c_head, 1)
            act.wait_ge(k_ready, 2)
            for h in range(5, 8):
                sc.activation(kbd_v[:, h, :, 0, :], ks_v[:, :, 0, :], ACT.Copy, scale=hmask[:, h:h + 1]
                              ).then_inc(kbd_ready_act, 1)
            act.wait_ge(bqs_ready, 1)
            act.wait_ge(qbd_zero, 1)
            act.wait_ge(q_ps, 2)
            for h in range(2):
                for a in range(2):
                    q = slice(64 * a, 64 * a + 64)
                    sc.activation(qbd[q, 1, h * XH:h * XH + XH, a, :],
                                  p7[q, 256 * h:256 * h + 256].rearrange("p (n i) -> p n i", n=XH),
                                  ACT.Identity, bias=bqs[q, 1:2], scale=SCALE).then_inc(qbd_ready_act, 1)
            act.wait_ge(c_zero, 2)
            for t in range(2):
                act.wait_ge(v_ps, t + 1)
                src = pT2[:, 512 * t:512 * t + 512].rearrange("p (x q d) -> p x q d", q=2, d=D)
                dst = vbd[:, 2048 * t:2048 * t + 2048].rearrange("p (x w) -> p x w", w=64)
                for s in range(2):
                    for q in range(2):
                        at = 48 * q + 8 * s
                        sc.activation(dst[64 * s:64 * s + 64, :, at:at + 8], src[64 * s:64 * s + 64, :, q, :],
                                      ACT.Copy).then_inc(v_ready, 1)
            def later_keys(h):
                sc.activation(kbd_v[:, h, :, 1, :], ks_v[:, :, 1, :], ACT.Copy, scale=hmask[:, h:h + 1]
                              ).then_inc(kbd_ready_act, 1)

            act.wait_ge(ld_gate, 48)
            sc.activation(tgx[:, :], gx[:, :], ACT.Tanh).then_inc(tg_ready, 1)
            sc.activation(tgf[:, :], gf[:, :], ACT.Tanh).then_inc(tg_ready, 1)

            def exps(p):
                act.wait_ge(shifted, p + 1)
                sc.activation(pm[:, p % 2, :, :], pm[:, p % 2, :, :], ACT.Exp).then_inc(exped, 1)

            def x2T_out(p):
                act.wait_ge(x2T_ps, p + 1)
                sc.activation(xn2T[:, p, :], X2T_PS[p], ACT.Copy).then_inc(x2T_ready, 1)

            def probs_out(p):
                if p >= 2:
                    act.wait_ge(o_ps, p - 1)
                for h in range(2):
                    act.wait_ge(pT_ps, 2 * p + h + 1)
                    sc.activation(pT[:, p % 2, 512 * h:512 * h + 512], pT2[:, 512 * h:512 * h + 512],
                                  ACT.Copy).then_inc(pT_ready, 1)

            for p in range(NP + 5):
                if 1 <= p <= NP:
                    probs_out(p - 1)
                if p >= 5:
                    x2T_out(p - 5)
                if p < NP:
                    exps(p)
                if p in (0, 1):
                    for h in (4 + 2 * p, 5 + 2 * p):
                        later_keys(h)
            act.wait_ge(dl_ready, 1)
            sc.activation(ex[:, :], dl[:, :], ACT.Exp).then_inc(ex_ready, 1)
            act.wait_ge(tg_ready, 2)
            sc.activation(warm[:, :], tgf[:, :], ACT.Silu)
            for n in range(0, NP, 2):
                act.wait_ge(xe_ps, n + 1)
                sc.activation(xe[:, :, n, :], BANKS[n % 4][:, 0:PS].rearrange("c (e s) -> c e s", e=E),
                              ACT.Copy).then_inc(xe_ready_act, 1)

            def hidden(m):
                e, c = divmod(m, FC)
                act.wait_ge(hg_ps, m + 1)
                if m >= 2:
                    act.wait_ge(u_ready, m - 1)
                sc.activation(hs[:, m % 2, :], pS[m % 2][:, 0:ES], ACT.Identity,
                              bias=bfc_sb[:, e, c:c + 1]).then_inc(h_ready, 1)

            def silu(m):
                act.wait_ge(u_ready, m + 1)
                sc.activation(z[:, m % 3, :], hg[:, m % 2, :], ACT.Silu).then_inc(z_ready, 1)

            def expert_out(e):
                gr = min(e // 3, 2)
                k = e - GROUPS[gr][0]
                act.wait_ge(f_ps, e + 1)
                sc.activation(oT[:, gr, :, k * SLOTS:(k + 1) * SLOTS],
                              pT2[:, 0:ES].rearrange("c (n s) -> c n s", n=NP), ACT.Identity,
                              bias=bp_sb[:, e:e + 1]).then_inc(oT_ready, 1)

            M = E * FC
            for m in range(M + 3):
                if m >= FC + 2 and m % FC == 2:
                    expert_out(m // FC - 1)
                if m < M:
                    hidden(m)
                if 1 <= m <= M:
                    silu(m - 1)

        @block.vector
        def _(dve):
            v = nc.vector
            n = [0]

            def then(ins):
                link(dve, dve_chain, n, ins)

            def norm_stats(src, st, m_v, k):
                then(v.bn_stats(st[:, k, :], src[:, k, :]))
                return v.bn_aggr(m_v[:, k, :], st[:, k, :])

            v.memset(penalty[:, :, :], 0.0).then_inc(dve_chain, 1)
            n[0] += 1
            v.memset(qbd[:, :, :, :, :], 0.0).then_inc(qbd_zero, 1)
            for h in range(2):
                dve.wait_ge(ld_x[h], 16)
                for k in range(h * XH, (h + 1) * XH):
                    v.bn_stats(stats[:, k, :], x_sb[:, k, :]).then_inc(dve_chain, 1)
                n[0] += XH
                dve.wait_ge(dve_chain, n[0])
                for k in range(h * XH, (h + 1) * XH):
                    last = v.bn_aggr(mv[:, k, :], stats[:, k, :])
                    if k < (h + 1) * XH - 1:
                        last.then_inc(dve_chain, 1)
                        n[0] += 1
                last.then_inc(var_ready, 1)
            for h in range(2):
                dve.wait_ge(rstd_ready, h + 1)
                for k in range(h * XH, (h + 1) * XH):
                    last = v.tensor_scalar(xn[:, k, :], x_sb[:, k, :], mv[:, k, 0:1], rstd[:, k:k + 1],
                                           ALU.subtract, ALU.mult)
                last.then_inc(xn_ready, 1)
            dve.wait_ge(bT_ready, 1)
            v.tensor_scalar(bqs[:, :], bq_sb, SCALE, None, ALU.mult).then_inc(bqs_ready, 1)
            dve.wait_ge(k_ps, 2)
            v.tensor_scalar(ks[:, 512:1024], BANKS[3], bk_sb[:, 1:2], None, ALU.add).then_inc(k_ready, 1)
            dve.wait_ge(xT_ps, 1)
            v.tensor_copy(xnT[:, 0:512], pT2[:, 0:512]).then_inc(xT_ready, 1)
            dve.wait_ge(c_head, 1)
            dve.wait_ge(k_ready, 2)
            for h in range(0, 5):
                v.tensor_scalar(kbd_v[:, h, :, 0, :], ks_v[:, :, 0, :], hmask[:, h:h + 1], None, ALU.mult
                                ).then_inc(kbd_ready_dve, 1)
            dve.wait_ge(ld_mask, 64)
            for a in range(2):
                v.tensor_scalar(penalty[32 * a:32 * a + 1, :, :], mask_u8[32 * a:32 * a + 1, :, :], MASKED, None,
                                ALU.mult).then_inc(pen_ready, 1)
            dve.wait_ge(qbd_zero, 1)
            dve.wait_ge(q_ps, 1)
            for h in range(2):
                for a in range(2):
                    q = slice(64 * a, 64 * a + 64)
                    v.tensor_scalar(qbd[q, 0, h * XH:h * XH + XH, a, :],
                                    p6[q, 256 * h:256 * h + 256].rearrange("p (n i) -> p n i", n=XH),
                                    bq_sb[q, 0:1], SCALE, ALU.add, ALU.mult).then_inc(qbd_ready_dve, 1)
            v.tensor_copy(bvm[:, :], bv_sb.broadcast_to([C, P])).then_inc(bvm_ready, 1)
            then(v.tensor_reduce(nmask[:, :], mask_nat[:, :, :], AX_X, ALU.add))
            then(v.tensor_scalar(live[:, :], nmask[:, :], -1.0, float(T), ALU.mult, ALU.add))
            then(v.reciprocal(rlive[:, :], live[:, :]))
            then(v.tensor_tensor(nmask[:, :], live[:, :], rlive[:, :], ALU.mult))
            v.tensor_tensor(nanfix[:, :], nmask[:, :], nmask[:, :], ALU.subtract).then_inc(nan_ready, 1)

            def shift(p):
                dve.wait_ge(s_ps, p + 1)
                sv = pS[p % 2][:, :].rearrange("p (h j) -> p h j", h=H)
                then(v.tensor_reduce(negmax[:, p, :], sv, AX_X, ALU.max, negate=True))
                if p >= 2:
                    dve.wait_ge(pT_ps, 2 * (p - 1))
                v.tensor_tensor(pm[:, p % 2, :, :], sv, negmax[:, p, :].unsqueeze(2).broadcast_to([P, H, T]),
                                ALU.add).then_inc(shifted, 1)

            def attention_out(p):
                dve.wait_ge(o_ps, p + 1)
                then(v.reciprocal(rden[:, p % 2, :], p6[:, P:2 * P]))
                if p >= 2:
                    dve.wait_ge(y_ps, p - 1)
                v.tensor_tensor(aT[:, p % 2, :], p6[:, 0:P], rden[:, p % 2, :], ALU.mult).then_inc(aT_ready, 1)

            def normalise_late(p):
                dve.wait_ge(rstd2_late, p + 1 - LATE)
                v.tensor_scalar(xn2[:, p, :], x2[:, p, :], mv2[:, p, 0:1], rstd2[:, p:p + 1],
                                ALU.subtract, ALU.mult).then_inc(xn2_late, 1)

            def best(p):
                if p == 0:
                    dve.wait_ge(ld_router, 32)
                dve.wait_ge(lg_ps, p + 1)
                v.tensor_tensor(lg[:, p, :], LG_PS[p], rb_bc[:, :], ALU.add).then_inc(lg_read, 1)
                dve.wait_ge(lg_read, p + 1)
                then(v.max(mx[:, p, :], lg[:, p, :]))
                v.max_index(ix[:, p, :], mx[:, p, :], lg[:, p, :]).then_inc(dve_chain, 1)
                n[0] += 1

            def residual(p):
                if p == 0:
                    dve.wait_ge(xb_ready, 1)
                    dve.wait_ge(tg_ready, 2)
                dve.wait_ge(y_ps, p + 1)
                v.scalar_tensor_tensor(out=x2[:, p, :], in0=p7[:, 0:C], scalar=tgx[:, 0:1], in1=xb[:, p, :],
                                       op0=ALU.mult, op1=ALU.add).then_inc(x2_ready, 1)
                dve.wait_ge(x2_ready, p + 1)
                norm_stats(x2, stats2, mv2, p).then_inc(x2_stats, 1)

            for p in range(NP + 6):
                if p >= 6:
                    best(p - 6)
                if p < NP:
                    shift(p)
                if p == 1:
                    dve.wait_ge(bvy_ps, 1)
                    dve.wait_ge(ld_gate, 48)
                    v.tensor_tensor(bias_y[:, :], p7[:, 0:C], bout_bc[:, :], ALU.add).then_inc(bias_y_ready, 1)
                if 3 <= p < NP + 3:
                    residual(p - 3)
                if LATE + 4 <= p < NP + 4:
                    normalise_late(p - 4)
                if 2 <= p < NP + 2:
                    attention_out(p - 2)
            dve.wait_ge(dve_chain, n[0])
            dve.wait_ge(c_route, 5)
            then(v.tensor_copy(idf[:, :, :].rearrange("p k n -> p n k"), ix[:, :, 0:2]))
            for k in range(2):
                v.tensor_tensor(oh[:, k, :, :], iota_e[:, :].unsqueeze(1).broadcast_to([P, NP, E]),
                                idf[:, k, :].unsqueeze(2).broadcast_to([P, NP, E]), ALU.is_equal
                                ).then_inc(oh_ready, 1)
            v.tensor_tensor(dl[:, :], mx[:, :, 1], mx[:, :, 0], ALU.subtract).then_inc(dl_ready, 1)
            dve.wait_ge(pos_ps, 1)
            dve.wait_ge(oh_ready, 2)
            cnt = [p6[:, k * NP * E:(k + 1) * NP * E].rearrange("p (n e) -> p n e", n=NP) for k in range(2)]
            v.scalar_tensor_tensor(out=pos0[:, :, :].rearrange("p n e -> p (n e)"), in0=p6[:, 0:NP * E], scalar=1.0,
                                   in1=oh[:, 0, :, :].rearrange("p n e -> p (n e)"),
                                   op0=ALU.add, op1=ALU.mult).then_inc(dve_chain, 1)
            v.scalar_tensor_tensor(out=pos1[:, :, :].rearrange("p n e -> p (n e)"), in0=p6[:, NP * E:2 * NP * E],
                                   scalar=1.0, in1=oh[:, 1, :, :].rearrange("p n e -> p (n e)"),
                                   op0=ALU.add, op1=ALU.mult).then_inc(dve_chain, 1)
            n[0] += 2
            dve.wait_ge(dve_chain, n[0])
            then(v.tensor_tensor(slot[:, :, :], pos0[:, :, :], pos1[:, :, :], ALU.add))
            dve.wait_ge(disp_zero, 2)
            for h in range(2):
                for a in range(2):
                    q = slice(64 * a, 64 * a + 64)
                    dvw = disp[q, h * XH:h * XH + XH, :].rearrange("p n (e a s) -> p (n e) a s", a=2, s=CAP)
                    v.tensor_tensor(dvw[:, :, a, :],
                                    slot[q, h * XH:h * XH + XH, :].rearrange("p n e -> p (n e)").unsqueeze(2)
                                    .broadcast_to([T, XH * E, CAP]),
                                    iota_s[q, :].unsqueeze(1).broadcast_to([T, XH * E, CAP]), ALU.is_equal
                                    ).then_inc(disp_ready, 1)
            for i in range(1, NP, 2):
                dve.wait_ge(xe_ps, i + 1)
                v.tensor_copy(xe[:, :, i, :], BANKS[i % 4][:, 0:PS].rearrange("c (e s) -> c e s", e=E)
                              ).then_inc(xe_ready_dve, 1)
            def gate(m):
                e, c = divmod(m, FC)
                dve.wait_ge(h_ready, m + 1)
                if m >= 2:
                    dve.wait_ge(z_ready, m - 1)
                v.scalar_tensor_tensor(out=hg[:, m % 2, :], in0=pS[m % 2][:, 512:512 + ES],
                                       scalar=bg_sb[:, e, c:c + 1], in1=hs[:, m % 2, :],
                                       op0=ALU.add, op1=ALU.mult).then_inc(u_ready, 1)

            def coll_out(i):
                gr, h = divmod(i, 2)
                w = GROUPS[gr][1] * SLOTS
                dve.wait_ge(cT2_ps, i + 1)
                v.tensor_copy(collT[0:w, gr, 4 * h:4 * h + 4, :].rearrange("s n t -> s (n t)"),
                              pT2[0:w, 512:1024]).then_inc(collT_ready, 1)

            def slots_out(i):
                gr, h = divmod(i, 2)
                w = GROUPS[gr][1] * SLOTS
                dve.wait_ge(os_ps, i + 1)
                if i >= 2:
                    dve.wait_ge(yf_ps, i - 1)
                v.tensor_copy(osl[0:w, i % 2, :, :].rearrange("s n c -> s (n c)"),
                              OS_PS[i][0:w, :]).then_inc(os_ready, 1)

            def weights():
                dve.wait_ge(ex_ready, 1)
                then(v.tensor_scalar(den[:, :], ex[:, :], 1.0, None, ALU.add))
                then(v.reciprocal(pr[:, 0, :], den[:, :]))
                then(v.tensor_tensor(pr[:, 1, :], ex[:, :], pr[:, 0, :], ALU.mult))
                for k, w in ((0, pw0), (1, pw1)):
                    v.tensor_tensor(w[:, :, :], oh[:, k, :, :],
                                    pr[:, k, :].unsqueeze(2).broadcast_to([P, NP, E]), ALU.mult
                                    ).then_inc(dve_chain, 1)
                v.tensor_scalar(slotc[:, :, :], slot[:, :, :], float(CAP), None, ALU.min).then_inc(dve_chain, 1)
                n[0] += 3
                dve.wait_ge(dve_chain, n[0])
                then(v.tensor_tensor(pw[:, :, :], pw0[:, :, :], pw1[:, :, :], ALU.add))

            def reads_of(a):
                q = slice(64 * a, 64 * a + 64)
                cv = coll[q, :, :].rearrange("p n (e a s) -> p (n e) a s", a=2, s=CAP)[:, :, a, :]
                v.tensor_tensor(cv, slotc[q, :, :].rearrange("p n e -> p (n e)").unsqueeze(2)
                                .broadcast_to([T, NP * E, CAP]),
                                iota_s[q, :].unsqueeze(1).broadcast_to([T, NP * E, CAP]), ALU.is_equal
                                ).then_inc(slot_ready, 1)

            M = E * FC
            after = {10: ("c", 0), 11: ("c", 1), 12: ("c", 2), 13: ("c", 3), 14: ("c", 4), 15: ("c", 5),
                     16: ("o", 0), 17: ("o", 1), 27: ("o", 2), 28: ("o", 3)}
            for m in range(M):
                gate(m)
                if m == 1:
                    weights()
                if m in (2, 4):
                    reads_of((m - 2) // 2)
                if m in after:
                    kind, i = after[m]
                    (coll_out if kind == "c" else slots_out)(i)
            slots_out(4)
            slots_out(5)
            for h in range(2):
                dve.wait_ge(yf_ps, 5 + h)
                v.scalar_tensor_tensor(out=fin[:, 4 * h:4 * h + 4, :].rearrange("p n c -> p (n c)"),
                                       in0=(p6, p7)[h][:, :], scalar=tgf[:, 0:1],
                                       in1=x2[:, 4 * h:4 * h + 4, :].rearrange("p n c -> p (n c)"),
                                       op0=ALU.mult, op1=ALU.add).then_inc(fin_ready, 1)


_INS = ["x", "ctx_1024", "mask_BxS2_bf0", "g_xattn", "g_ffn", "L0_xattn_Wq", "L0_xattn_bq", "L0_xattn_Wkv",
        "L0_xattn_bkv", "L0_xattn_Wout", "L0_xattn_bout", "L0_ffn_router_w", "L0_ffn_router_b",
        "L0_ffn_w_c_fc", "L0_ffn_b_c_fc", "L0_ffn_w_gate", "L0_ffn_b_gate", "L0_ffn_w_c_proj",
        "L0_ffn_b_c_proj"]
_OUTS = [((16, 64, 128), "float32")]


def kernel(**inputs):
    import numpy as _np
    import concourse.bacc as _bacc
    from concourse import mybir as _mybir
    from concourse.bass_utils import run_bass_kernel_spmd as _run

    nc = _bacc.Bacc("TRN2", target_bir_lowering=False, num_devices=1)
    arrays, args = {}, []
    for name in _INS:
        a = _np.ascontiguousarray(inputs[name])
        arrays[f"in_{name}_dram"] = a
        args.append(nc.dram_tensor(f"in_{name}_dram", a.shape, _mybir.dt.from_np(a.dtype), kind="ExternalInput").ap())
    for i, (shape, dtype) in enumerate(_OUTS):
        dt = _mybir.dt.from_np(_np.dtype(dtype))
        args.append(nc.dram_tensor(f"out_{i}_dram", shape, dt, kind="ExternalOutput").ap())
    gated_attention_moe(nc, *args)
    r = _run(nc, [arrays], core_ids=[0])
    got = tuple(r.results[0][f"out_{i}_dram"] for i in range(len(_OUTS)))
    return got[0]
```

```python
from contextlib import ExitStack

import concourse.bass as bass
from concourse import mybir

F32 = mybir.dt.float32
F32R = mybir.dt.float32r
BF16 = mybir.dt.bfloat16
U8 = mybir.dt.uint8
U32 = mybir.dt.uint32
ALU = mybir.AluOpType
ACT = mybir.ActivationFunctionType
AX_X = mybir.AxisListType.X

EPS = 1e-5
MASKED = -1.0e30
LOAD_FACTOR = 1.2
TOP_K = 2


def gated_attention_moe(nc, x, ctx_in, mask, g_xattn, g_ffn, wq, bq, wkv, bkv, wout, bout,
                        router_w, router_b, w_fc, b_fc, w_gate, b_gate, w_proj, b_proj, out):
    B, T, C = x.shape
    E = router_w.shape[1]
    F = w_fc.shape[2]
    H = 16
    D = C // H
    CAP = int(LOAD_FACTOR * TOP_K * T // E)
    P = 2 * T
    NP = B // 2
    HALF = C // 2
    HH = H // 2
    FC = F // 128
    SLOTS = 2 * CAP
    PS = E * SLOTS
    ES = B * CAP
    GROUPS = [(0, 3), (3, 3), (6, 2)]
    GW = 3 * SLOTS
    SCALE = float(D) ** -0.5
    assert P == 128 and C == 128 and D == 8 and NP == 8 and E == 8

    with ExitStack() as stack:
        def sb(name, shape, dt=F32):
            return stack.enter_context(nc.sbuf_tensor(name, shape, dt))

        def ps(name, shape):
            return stack.enter_context(nc.psum_tensor(name, shape, F32))

        def sem(name):
            return stack.enter_context(nc.semaphore(name))

        c_sb = sb("c_sb", [P, NP, C])
        xn = sb("xn", [P, NP, C])
        xnT = sb("xnT", [C, NP * P])
        wq_sb = sb("wq_sb", [C, C])
        wkv_sb = sb("wkv_sb", [C, 2 * C])
        wout_sb = sb("wout_sb", [C, C])
        b_rows = sb("b_rows", [77, 128])
        bT = sb("bT", [128, 77])
        bq_sb, bk_sb, bv_sb = bT[:, 72:74], bT[:, 74:76], bT[:, 76:77]
        bout_bc = sb("bout_bc", [P, C])
        bqs = sb("bqs", [P, 2])
        gx = sb("gx", [P, 1])
        gf = sb("gf", [P, 1])
        tgx = sb("tgx", [P, 1])
        tgf = sb("tgf", [P, 1])
        warm = sb("warm", [P, 1])
        rw_sb = sb("rw_sb", [C, E])
        rb_bc = sb("rb_bc", [P, E])
        mask_nat = sb("mask_nat", [P, NP, T], U8)
        mask_u8 = sb("mask_u8", [64, NP, T], U8)
        penalty = sb("penalty", [64, NP, T], BF16)
        batch_row = sb("batch_row", [64, P], BF16)
        nmask = sb("nmask", [P, NP])
        live = sb("live", [P, NP])
        rlive = sb("rlive", [P, NP])
        nanfix = sb("nanfix", [P, NP])
        w_hi_first = sb("w_hi_first", [128, E // 2, 2, F], F32R)
        with nc.sbuf_tensor("w_raw", [128, E, 2, F], F32) as w_raw:
            pass
        w_lo = sb("w_lo", [128, E, 2, F], F32R)
        wp_sb = sb("wp_sb", [128, E, FC, C])
        bfc_sb = bT[:, 0:E * FC].rearrange("p (e c) -> p e c", e=E)
        bg_sb = bT[:, E * FC:2 * E * FC].rearrange("p (e c) -> p e c", e=E)
        bp_sb = bT[:, 2 * E * FC:2 * E * FC + E]
        ident = sb("ident", [128, 128])
        hmask = sb("hmask", [P, HH])
        before = sb("before", [P, P], BF16)
        same = sb("same", [P, P], BF16)
        iota_e = sb("iota_e", [P, E])
        iota_s = sb("iota_s", [P, CAP])
        mhalf = sb("mhalf", [P, NP])
        stats = sb("stats", [P, NP, 6])
        mv = sb("mv", [P, NP, 2])
        veps = sb("veps", [P, NP])
        rstd = sb("rstd", [P, NP])
        stats2 = sb("stats2", [P, NP, 6])
        mv2 = sb("mv2", [P, NP, 2])
        veps2 = sb("veps2", [P, NP])
        rstd2 = sb("rstd2", [P, NP])
        negmax = sb("negmax", [P, NP, H])
        ones_q = sb("ones_q", [P, 2, 32])
        rden = sb("rden", [C, 2, P])
        bvm = sb("bvm", [C, P])
        bias_y = sb("bias_y", [P, C])
        aT = sb("aT", [C, 2, P])
        tb = sb("tb", [P, C])
        x2 = sb("x2", [P, NP, C])
        xn2 = xn
        xn2T = xnT[:, :].rearrange("c (n t) -> c n t", n=NP)
        lg = sb("lg", [P, NP, E])
        mx = sb("mx", [P, NP, 8])
        ix = sb("ix", [P, NP, 8], U32)
        idf = sb("idf", [P, 2, NP])
        oh = sb("oh", [P, 2, NP, E], BF16)
        pos0 = sb("pos0", [P, NP, E])
        pos1 = sb("pos1", [P, NP, E])
        slot = sb("slot", [P, NP, E])
        slotc = sb("slotc", [P, NP, E])
        dl = sb("dl", [P, NP])
        ex = sb("ex", [P, NP])
        den = sb("den", [P, NP])
        pr = sb("pr", [P, 2, NP])
        pw0 = sb("pw0", [P, NP, E])
        pw1 = sb("pw1", [P, NP, E])
        pw = sb("pw", [P, NP, E])
        with ExitStack() as attention:
            def early(name, shape, dt=F32):
                return attention.enter_context(nc.sbuf_tensor(name, shape, dt))

            disp = early("disp", [P, NP, PS], F32R)
            xn2_hi = early("xn2_hi", [P, NP, C], F32R)
            xn2_lo = early("xn2_lo", [P, NP, C], F32R)
            kbd = early("kbd", [P, HH, 2 * NP * T])
            qbd = early("qbd", [P, 2, NP, 2, T])
            ks = early("ks", [P, 2 * NP * T])
            cT = early("cT", [C, NP * P])
            x_sb = early("x_sb", [P, NP, C])
            pm = early("pm", [P, 2, H, T])
            pT = early("pT", [P, 2, HH * P])
            vbd = early("vbd", [P, B * HH * 32])
        collT = sb("collT", [128, 3, NP, P])
        osl = sb("osl", [128, 2, 4, C])
        hs = sb("hs", [128, 2, ES])
        w_hi_last = sb("w_hi_last", [128, E // 2, 2, F], F32R)
        coll = sb("coll", [P, NP, PS])
        oT = sb("oT", [C, 3, NP, GW])
        xe_hi = sb("xe_hi", [C, E, NP, SLOTS], F32R)
        xe_lo = sb("xe_lo", [C, E, NP, SLOTS], F32R)
        hg = sb("hg", [128, 2, ES])
        z = sb("z", [128, 3, ES])

        def w_hi(e, k):
            return (w_hi_first, w_hi_last)[e // (E // 2)][:, e % (E // 2), k, :]

        xb = x_sb
        fin = c_sb

        pS = [ps(f"pS{r}", [128, 1024]) for r in range(2)]
        pT2 = ps("pT2", [128, 1024])
        p6 = ps("p6", [128, 512])
        p7 = ps("p7", [128, 512])
        OS_PS = [pT2[:, 512:1024]] * 5 + [pS[0][:, 0:512]]
        LATE = 4
        DVE_NORM = 5
        BANKS = [pS[0][:, 0:512], pS[0][:, 512:1024], pS[1][:, 0:512], pS[1][:, 512:1024]]

        X2T_PS = [p6[:, 2 * P:3 * P]] * LATE + [BANKS[p % 2][:, 0:P] for p in range(LATE, NP)]
        LG_PS = [(p7[:, C + p * E:C + (p + 1) * E] if p < LATE else BANKS[2][:, (p - LATE) * E:(p - LATE + 1) * E])
                 for p in range(NP)]
        O_PS = [p6[:, 0:2 * P]] * (NP - 1) + [BANKS[3][:, 0:2 * P]]
        Y_PS = [p7[:, 0:C]] * (NP - 1) + [BANKS[2][:, 0:C]]
        IDLE = pT2[:, 512:1024]
        COUNT_PS = [pT2[:, 0:512], BANKS[0]]
        XE_PS = [(pT2[:, 0:512], BANKS[3]), (p6[:, :], p7[:, :]), (BANKS[1], BANKS[2]), (pT2[:, 0:512], BANKS[3]),
                 (BANKS[0], pT2[:, 512:1024]), (p6[:, :], p7[:, :]), (BANKS[1], BANKS[2]), (pT2[:, 0:512], BANKS[3])]

        ld_x = [sem(f"ld_x{h}") for h in range(2)]
        ld_ctx = [sem(f"ld_ctx{h}") for h in range(2)]
        ld_wq = sem("ld_wq")
        ld_wkv = sem("ld_wkv")
        ld_bias = sem("ld_bias")
        ld_gate = sem("ld_gate")
        ld_mask = sem("ld_mask")
        ld_wout = sem("ld_wout")
        ld_router = sem("ld_router")
        bT_ps = sem("bT_ps")
        bT_ready = sem("bT_ready")
        ld_exp = [sem(f"ld_exp{e}") for e in range(E)]
        st_out = sem("st_out")
        pool_chain = sem("pool_chain")
        dve_chain = sem("dve_chain")
        c_ident = sem("c_ident")
        c_head = sem("c_head")
        c_pair = sem("c_pair")
        c_route = sem("c_route")
        c_zero = sem("c_zero")
        c_quarter = sem("c_quarter")
        pen_ready = sem("pen_ready")
        var_ready = sem("var_ready")
        rstd_ready = sem("rstd_ready")
        xn_ready = sem("xn_ready")
        cT_ps = sem("cT_ps")
        cT_ready = sem("cT_ready")
        xT_ps = sem("xT_ps")
        xT_ready = sem("xT_ready")
        k_ps = sem("k_ps")
        k_ready = sem("k_ready")
        q_ps = sem("q_ps")
        v_ps = sem("v_ps")
        v_ready = sem("v_ready")
        kbd_ready_act = sem("kbd_ready_act")
        kbd_ready_dve = sem("kbd_ready_dve")
        kbd_ready_pool = sem("kbd_ready_pool")
        qbd_ready_act = sem("qbd_ready_act")
        qbd_ready_dve = sem("qbd_ready_dve")
        qbd_zero = sem("qbd_zero")
        bqs_ready = sem("bqs_ready")
        s_ps = sem("s_ps")
        shifted = sem("shifted")
        exped = sem("exped")
        bvm_ready = sem("bvm_ready")
        bvy_ps = sem("bvy_ps")
        bias_y_ready = sem("bias_y_ready")
        nan_ready = sem("nan_ready")
        lg_read = sem("lg_read")
        x2_stats = sem("x2_stats")
        disp_zero = sem("disp_zero")
        xe_ready_act = sem("xe_ready_act")
        xe_ready_dve = sem("xe_ready_dve")
        w_hi_ready = sem("w_hi_ready")
        w_lo_ready = sem("w_lo_ready")
        xn2_hi_ready = sem("xn2_hi_ready")
        xn2_lo_ready = sem("xn2_lo_ready")
        coll_zero = sem("coll_zero")
        pT_ps = sem("pT_ps")
        pT_ready = sem("pT_ready")
        o_ps = sem("o_ps")
        aT_ready = sem("aT_ready")
        y_ps = sem("y_ps")
        x2_ready = sem("x2_ready")
        xb_ready = sem("xb_ready")
        tg_ready = sem("tg_ready")
        xn2_ready = sem("xn2_ready")
        rstd2_late = sem("rstd2_late")
        xn2_late = sem("xn2_late")
        x2T_ps = sem("x2T_ps")
        x2T_ready = sem("x2T_ready")
        lg_ps = sem("lg_ps")
        oh_ready = sem("oh_ready")
        pos_ps = sem("pos_ps")
        dl_ready = sem("dl_ready")
        ex_ready = sem("ex_ready")
        disp_ready = sem("disp_ready")
        slot_ready = sem("slot_ready")
        coll_ready = sem("coll_ready")
        xe_ps = sem("xe_ps")
        hg_ps = sem("hg_ps")
        h_ready = sem("h_ready")
        u_ready = sem("u_ready")
        z_ready = sem("z_ready")
        f_ps = sem("f_ps")
        oT_ready = sem("oT_ready")
        cT2_ps = sem("cT2_ps")
        collT_ready = sem("collT_ready")
        os_ps = sem("os_ps")
        os_ready = sem("os_ready")
        os_ready_act = sem("os_ready_act")
        yf_ps = sem("yf_ps")
        fin_ready = sem("fin_ready")

        x_v = x.rearrange("(n a) i c -> (a i) n c", a=2)
        c_v = ctx_in.rearrange("(n a) i c -> (a i) n c", a=2)
        out_v = out.rearrange("(n a) i c -> (a i) n c", a=2)
        XH = NP // 2
        ACT_UNITS = [0, 0, 0, 1, 3, 5, 7, 8]
        POOL_UNITS = [0, 1, 2, 3, 4, 4, 4, 4]

        TURN_COLL_AT = [13, 14, 15, 16, 17, 18]
        TURN_OUT_AT = [20, 21, 27, 28]
        COLLECT_AT = [21, 23, 28, 29]

        ks_v = ks[:, :].rearrange("p (f g x) -> p f g x", f=2, g=2)
        kbd_v = kbd[:, :, :].rearrange("p h (f g x) -> p h f g x", f=2, g=2)

        def row(v):
            return v.rearrange("(o c) -> o c", o=1)

        def link(eng, chain, count, ins):
            count[0] += 1
            ins.then_inc(chain, 1)
            eng.wait_ge(chain, count[0])

        block = stack.enter_context(nc.Block())

        @block.sync
        def _(sp):
            for h in range(2):
                sp.dma_start(x_sb[:, h * XH:(h + 1) * XH, :], x_v[:, h * XH:(h + 1) * XH, :]).then_inc(ld_x[h], 16)
            sp.dma_start(b_rows[0:32, :], b_fc.rearrange("e o (c p) -> (e o c) p", p=128)).then_inc(ld_bias, 16)
            sp.dma_start(b_rows[32:64, :], b_gate.rearrange("e o (c p) -> (e o c) p", p=128)).then_inc(ld_bias, 16)
            sp.dma_start(b_rows[64:72, :], b_proj.rearrange("e o c -> (e o) c")).then_inc(ld_bias, 16)
            for at, vec in ((72, bq), (74, bkv[0:C])):
                sp.dma_start(b_rows[at:at + 2, :].rearrange("f (a r) -> f a r", a=2),
                             vec.rearrange("(f a r) -> f a r", f=2, a=1).broadcast_to([2, 2, HALF])
                             ).then_inc(ld_bias, 16)
            sp.dma_start(b_rows[76:77, :], row(bkv[C:2 * C])).then_inc(ld_bias, 16)
            for a in range(2):
                sp.dma_start(mask_nat[64 * a:64 * a + 64, :, :],
                              mask.rearrange("(o n a) j -> o a n j", a=2, o=1)[:, a].broadcast_to([64, NP, T])
                              ).then_inc(ld_mask, 16)
                sp.dma_start(mask_u8[32 * a:32 * a + 1, :, :],
                              mask.rearrange("(o n a) j -> o a n j", a=2, o=1)[:, a]).then_inc(ld_mask, 16)
            sp.dma_start(wout_sb[:, :], wout).then_inc(ld_wout, 16)
            sp.dma_start(bout_bc[:, :], row(bout).broadcast_to([P, C])).then_inc(ld_gate, 16)
            sp.dma_start(gx[:, :], row(g_xattn).broadcast_to([P, 1])).then_inc(ld_gate, 16)
            sp.dma_start(gf[:, :], row(g_ffn).broadcast_to([P, 1])).then_inc(ld_gate, 16)
            sp.dma_start(rw_sb[:, :], router_w).then_inc(ld_router, 16)
            sp.dma_start(rb_bc[:, :], row(router_b).broadcast_to([P, E])).then_inc(ld_router, 16)
            for e in range(E):
                sp.dma_start(w_raw[:, e, 0, :], w_fc[e]).then_inc(ld_exp[e], 16)
                sp.dma_start(w_raw[:, e, 1, :], w_gate[e]).then_inc(ld_exp[e], 16)
                sp.dma_start(wp_sb[:, e, :, :], w_proj[e].rearrange("(c p) o -> p c o", p=128)).then_inc(ld_exp[e], 16)
            for i, (lo, hi) in enumerate(((0, 4), (4, 6), (6, 8))):
                sp.wait_ge(fin_ready, i + 1)
                sp.dma_start(out_v[:, lo:hi, :], fin[:, lo:hi, :]).then_inc(st_out, 16)
            sp.wait_ge(st_out, 48)

        @block.gpsimd
        def _(pool):
            n = [0]
            g = nc.gpsimd

            def then(ins):
                link(pool, pool_chain, n, ins)

            then(g.memset(ident[:, :], 0.0))
            g.affine_select(out=ident[:, :], in_=ident[:, :], compare_op=ALU.not_equal, fill=1.0, base=0,
                            pattern=[[-1, 128]], channel_multiplier=1).then_inc(c_ident, 1)
            then(g.memset(hmask[:, :], 1.0))
            for a in range(2):
                part = hmask[64 * a:64 * a + 64, :]
                then(g.affine_select(out=part, in_=part, compare_op=ALU.is_ge, fill=0.0, base=0,
                                     pattern=[[-D, HH]], channel_multiplier=1))
                then(g.affine_select(out=part, in_=part, compare_op=ALU.is_ge, fill=0.0, base=D - 1,
                                     pattern=[[D, HH]], channel_multiplier=-1))
            g.memset(mhalf[:, :], -0.5).then_inc(c_head, 1)
            g.memset(vbd[:, 0:B * HH * 16], 0.0).then_inc(c_zero, 1)
            for h in range(2):
                lo, hi = h * XH, (h + 1) * XH
                pool.wait_ge(var_ready, h + 1)
                then(g.tensor_scalar(veps[:, lo:hi], mv[:, lo:hi, 1], EPS, None, ALU.add))
                g.tensor_tensor(rstd[:, lo:hi], veps[:, lo:hi], mhalf[:, lo:hi], ALU.pow).then_inc(rstd_ready, 1)
            g.memset(vbd[:, B * HH * 16:], 0.0).then_inc(c_zero, 1)
            then(g.memset(batch_row[:, :], 0.0))
            g.memset(batch_row[0:1, 0:T], 1.0).then_inc(c_pair, 1)
            pool.wait_ge(c_pair, 1)
            g.memset(batch_row[32:33, T:P], 1.0).then_inc(c_pair, 1)
            pool.wait_ge(c_pair, 2)
            then(g.memset(ones_q[:, :, :], 0.0))
            for i, (a, q) in enumerate(((0, 0), (0, 1), (1, 0), (1, 1))):
                at = 16 * q + 8 * a
                g.memset(ones_q[64 * a:64 * a + 64, q, at:at + 8], 1.0).then_inc(c_quarter, 1)
                pool.wait_ge(c_quarter, i + 1)
            pool.wait_ge(k_ready, 2)
            for h in range(0, 4):
                g.tensor_scalar(kbd_v[:, h, :, 1, :], ks_v[:, :, 1, :], hmask[:, h:h + 1], None, ALU.mult
                                ).then_inc(kbd_ready_pool, 1)
            pool.wait_ge(nan_ready, 1)
            then(g.tensor_tensor(xb[:, :, :], x_sb[:, :, :], nanfix[:, :].unsqueeze(2).broadcast_to([P, NP, C]),
                                 ALU.add))
            then(g.memset(before[:, :], 1.0))
            then(g.affine_select(out=before[:, :], in_=before[:, :], compare_op=ALU.is_gt, fill=0.0,
                                 base=0, pattern=[[1, P]], channel_multiplier=-1))
            g.memset(before[0:T, T:P], 0.0).then_inc(c_route, 1)
            pool.wait_ge(c_route, 1)
            then(g.memset(same[:, :], 1.0))
            g.memset(same[0:T, T:P], 0.0).then_inc(c_route, 1)
            pool.wait_ge(c_route, 2)
            g.memset(same[T:P, 0:T], 0.0).then_inc(c_route, 1)
            pool.wait_ge(c_route, 3)
            g.iota(iota_e[:, :], [[1, E]], base=0, channel_multiplier=0,
                   allow_small_or_imprecise_dtypes=True).then_inc(c_route, 1)
            g.iota(iota_s[:, :], [[1, CAP]], base=1, channel_multiplier=0,
                   allow_small_or_imprecise_dtypes=True).then_inc(c_route, 1)
            pool.wait_ge(bias_y_ready, 1)
            pool.wait_ge(tg_ready, 1)
            then(g.tensor_scalar(tb[:, :], bias_y[:, :], tgx[:, 0:1], None, ALU.mult))
            g.tensor_tensor(xb[:, :, :], xb[:, :, :], tb[:, :].unsqueeze(1).broadcast_to([P, NP, C]),
                            ALU.add).then_inc(xb_ready, 1)
            g.memset(disp[:, :, :].bitcast(F32), 0.0).then_inc(disp_zero, 1)

            def remainder(u):
                e, k = divmod(u, 2)
                pool.wait_ge(w_hi_ready, u + 1)
                g.tensor_tensor(w_lo[:, e, k, :], w_raw[:, e, k, :], w_hi(e, k).bitcast(F32), ALU.subtract
                                ).then_inc(w_lo_ready, 1)

            def remainder_x(h):
                pairs = slice(h * XH, (h + 1) * XH)
                pool.wait_ge(xn2_hi_ready, h + 1)
                g.tensor_tensor(xn2_lo[:, pairs, :], xn2[:, pairs, :], xn2_hi[:, pairs, :].bitcast(F32),
                                ALU.subtract).then_inc(xn2_lo_ready, 1)

            done = 0
            for p in range(NP):
                pool.wait_ge(x2_stats, p + 1)
                then(g.tensor_scalar(veps2[:, p:p + 1], mv2[:, p, 1:2], EPS, None, ALU.add))
                power = g.tensor_tensor(rstd2[:, p:p + 1], veps2[:, p:p + 1], mhalf[:, p:p + 1], ALU.pow)
                if p < DVE_NORM:
                    then(power)
                    g.tensor_scalar(xn2[:, p, :], x2[:, p, :], mv2[:, p, 0:1], rstd2[:, p:p + 1],
                                    ALU.subtract, ALU.mult).then_inc(xn2_ready, 1)
                else:
                    power.then_inc(rstd2_late, 1)
                for u in range(done, POOL_UNITS[p]):
                    remainder(u)
                done = POOL_UNITS[p]
                if p == NP - 3:
                    pool.wait_ge(s_ps, NP)
                    g.memset(coll[:, :, :], 0.0).then_inc(coll_zero, 1)
                    remainder_x(0)
            remainder_x(1)
            for u in range(done, 2 * E):
                remainder(u)

            def weigh(i):
                a, c = divmod(i, 4)
                pool.wait_ge(slot_ready, i // 2 + 1)
                q = slice(64 * a, 64 * a + 64)
                pairs = slice(2 * c, 2 * c + 2)
                cv = coll[q, pairs, :].rearrange("p n (e a s) -> p (n e) a s", a=2, s=CAP)[:, :, a, :]
                pv = pw[q, pairs, :].rearrange("p n e -> p (n e)").unsqueeze(2).broadcast_to([T, 2 * E, CAP])
                g.tensor_tensor(cv, cv, pv, ALU.mult).then_inc(coll_ready, 1)

            for i in range(8):
                if i >= 1:
                    pool.wait_ge(coll_ready, i)
                weigh(i)

        @block.tensor
        def _(pe):
            mm = nc.tensor.matmul

            def keep_busy(bank, times):
                for _ in range(times):
                    mm(bank[:, 0:128], ident[:, :], ident[:, :], start=True, stop=True)

            pe.wait_ge(c_ident, 1)
            keep_busy(BANKS[1], 7)
            for h in range(2):
                pe.wait_ge(ld_ctx[h], 16)
                for j in range(XH):
                    last = nc.tensor.transpose(pT2[:, 512 * h + 128 * j:512 * h + 128 * j + 128],
                                               c_sb[:, h * XH + j, :], ident[:, :])
                last.then_inc(cT_ps, 1)
                keep_busy(BANKS[1], 2)

            def turn_x(h):
                pe.wait_ge(cT_ready, h + 1)
                pe.wait_ge(xn_ready, h + 1)
                for j in range(XH):
                    last = nc.tensor.transpose(pT2[:, 512 * h + 128 * j:512 * h + 128 * j + 128],
                                               xn[:, h * XH + j, :], ident[:, :])
                last.then_inc(xT_ps, 1)

            cTv = cT[:, :].rearrange("c (n a j) -> c a n j", a=2, j=T)

            def keys(f):
                pe.wait_ge(cT_ready, 2)
                pe.wait_ge(ld_wkv, 16)
                for a in range(2):
                    last = mm(BANKS[2 + f][64 * a:64 * a + 64, :], wkv_sb[:, HALF * f:HALF * f + HALF],
                              cTv[:, a], start=True, stop=True, tile_position=(0, 64 * a))
                last.then_inc(k_ps, 1)

            turn_x(0)
            keys(0)
            turn_x(1)
            keys(1)
            pe.wait_ge(ld_bias, 16 * 6)
            nc.tensor.transpose(BANKS[0][:, 0:77], b_rows[:, :], ident[0:77, 0:77]).then_inc(bT_ps, 1)
            keep_busy(BANKS[1], 3)
            pe.wait_ge(xT_ready, 2)
            pe.wait_ge(ld_wq, 16)
            xTv = xnT[:, :].rearrange("c (n a j) -> c a n j", a=2, j=T)
            for f in range(2):
                for a in range(2):
                    last = mm((p6, p7)[f][64 * a:64 * a + 64, :], wq_sb[:, HALF * f:HALF * f + HALF],
                              xTv[:, a], start=True, stop=True, tile_position=(0, 64 * a))
                last.then_inc(q_ps, 1)

            kv = kbd[:, :, :].rearrange("p h (f n j) -> p f n h j", f=2, n=NP)

            def scores(p, f):
                if p >= 2 and f == 0:
                    pe.wait_ge(shifted, p - 1)
                if p == NP // 2 and f == 0:
                    pe.wait_ge(qbd_ready_dve, 4)
                    pe.wait_ge(qbd_ready_act, 4)
                    pe.wait_ge(kbd_ready_act, 7)
                    pe.wait_ge(kbd_ready_pool, 4)
                bank = pS[p % 2][:, 512 * f:512 * f + 512]
                mm(bank, batch_row[:, :], penalty[:, p, :].unsqueeze(1).broadcast_to([64, HH, T]),
                   start=True, stop=False)
                last = mm(bank, qbd[:, f, p, :, :].rearrange("p a i -> p (a i)"), kv[:, f, p],
                          start=False, stop=True)
                if f == 1:
                    last.then_inc(s_ps, 1)

            def transpose_probs(p):
                pe.wait_ge(exped, p + 1)
                for h in range(2):
                    if p == 0:
                        pe.wait_ge(v_ready, 4 * (h + 1))
                    else:
                        pe.wait_ge(pT_ready, 2 * (p - 1) + h + 1)
                    for m in range(4 * h, 4 * h + 4):
                        last = nc.tensor.transpose(
                            pT2[:, 128 * m:128 * m + 128],
                            pm[:, p % 2, 2 * m:2 * m + 2, :].rearrange("p h j -> p (h j)"), ident[:, :])
                    last.then_inc(pT_ps, 1)

            def weighted_values(p):
                pe.wait_ge(pT_ready, 2 * (p + 1))
                if p == 0:
                    pe.wait_ge(qbd_ready_dve, 4)
                elif p < NP - 1:
                    pe.wait_ge(aT_ready, p)
                if 3 <= p < NP - 1:
                    pe.wait_ge(x2T_ready, p - 2)
                for a in range(2):
                    for q in range(2):
                        for r in range(4):
                            at = (2 * p + a) * 256 + 64 * r + 32 * q
                            m = 2 * r + q
                            last = mm(O_PS[p][32 * r:32 * r + 32, a * T:(a + 1) * T], vbd[:, at:at + 32],
                                      pT[:, p % 2, m * 128 + a * T:m * 128 + (a + 1) * T],
                                      start=(q == 0), stop=(q == 1), tile_position=(0, 32 * r))
                for q in range(2):
                    for r in range(4):
                        m = 2 * r + q
                        last = mm(O_PS[p][32 * r:32 * r + 32, P:2 * P], ones_q[:, q, :],
                                  pT[:, p % 2, m * 128:m * 128 + 128],
                                  start=(q == 0), stop=(q == 1), tile_position=(0, 32 * r))
                last.then_inc(o_ps, 1)

            def turn_x2(p):
                if p < LATE:
                    pe.wait_ge(aT_ready, p + 3)
                    pe.wait_ge(xn2_ready, p + 1)
                else:
                    if p >= LATE + 2:
                        pe.wait_ge(x2T_ready, p - 1)
                    if p < DVE_NORM:
                        pe.wait_ge(xn2_ready, p + 1)
                    else:
                        pe.wait_ge(xn2_late, p + 1 - DVE_NORM)
                nc.tensor.transpose(X2T_PS[p], xn2[:, p, :], ident[:, :]).then_inc(x2T_ps, 1)

            def logits(p):
                pe.wait_ge(x2T_ready, p + 1)
                pe.wait_ge(x2_ready, p + 3 if p < LATE else NP)
                mm(LG_PS[p], xn2T[:, p, :], rw_sb[:, :], start=True, stop=True).then_inc(lg_ps, 1)

            def project(p):
                pe.wait_ge(aT_ready, p + 1)
                if 1 <= p < NP - 1:
                    pe.wait_ge(x2_ready, p)
                if p == NP - 2:
                    pe.wait_ge(lg_read, 1)
                mm(Y_PS[p], aT[:, p % 2, :], wout_sb[:, :], start=True, stop=True).then_inc(y_ps, 1)

            def values(t):
                for b in range(8 * t, 8 * t + 8):
                    for s in range(2):
                        last = mm(pT2[64 * s:64 * s + 64, b * 64:b * 64 + 64],
                                  cT[:, b * T:(b + 1) * T], wv[:, s], start=True, stop=True,
                                  tile_position=(0, 64 * s))
                last.then_inc(v_ps, 1)

            wv = wkv_sb[:, C:2 * C].rearrange("c (m s d) -> c s m d", s=2, d=D)
            values(0)
            pe.wait_ge(c_pair, 2)
            pe.wait_ge(pen_ready, 2)
            pe.wait_ge(bT_ready, 1)
            pe.wait_ge(qbd_ready_dve, 2)
            pe.wait_ge(qbd_ready_act, 2)
            pe.wait_ge(kbd_ready_act, 3)
            pe.wait_ge(kbd_ready_dve, 5)
            scores(0, 0)
            scores(0, 1)
            scores(1, 0)
            scores(1, 1)
            values(1)
            pe.wait_ge(qbd_ready_act, 4)
            pe.wait_ge(bvm_ready, 1)
            pe.wait_ge(ld_wout, 16)
            mm(p7[:, 0:C], bvm[:, :], wout_sb[:, :], start=True, stop=True).then_inc(bvy_ps, 1)
            pe.wait_ge(c_quarter, 4)
            pe.wait_ge(ld_router, 32)
            for p in range(NP + 1):
                if p >= NP - 1:
                    pe.wait_ge(shifted, NP - 1)
                    keep_busy(BANKS[1], 2)
                if 1 <= p < NP - 1:
                    scores(p + 1, 0)
                if p >= 1:
                    transpose_probs(p - 1)
                if p >= 5:
                    turn_x2(p - 5)
                if 1 <= p < NP - 1:
                    scores(p + 1, 1)
                if p >= 6:
                    logits(p - 6)
                if p >= 3:
                    if p == 3:
                        pe.wait_ge(bias_y_ready, 1)
                    project(p - 3)
                if p == NP:
                    keep_busy(BANKS[1], 2)
                if p >= 2:
                    weighted_values(p - 2)
            logits(3)
            weighted_values(NP - 1)
            keep_busy(IDLE, 4)
            project(NP - 2)
            turn_x2(4)
            keep_busy(IDLE, 4)
            project(NP - 1)

            def counts(g):
                pe.wait_ge(oh_ready, 2 * g + 2)
                pe.wait_ge(c_route, 5)
                first, second = (oh[:, k, g * XH:(g + 1) * XH, :].rearrange("p n e -> p (n e)") for k in range(2))
                w = XH * E
                mm(COUNT_PS[g][:, 0:w], before[:, :], first, start=True, stop=True)
                mm(COUNT_PS[g][:, w:2 * w], before[:, :], second, start=True, stop=False)
                mm(COUNT_PS[g][:, w:2 * w], same[:, :], first, start=False, stop=True).then_inc(pos_ps, 1)

            def dispatch(n):
                pe.wait_ge(disp_ready, 2 if n < XH else 4 if n < XH + 2 else 6)
                pe.wait_ge(xn2_hi_ready, n // XH + 1)
                pe.wait_ge(xn2_lo_ready, n // XH + 1)
                if n == 2:
                    pe.wait_ge(lg_read, 2)
                elif n == XH - 1:
                    pe.wait_ge(xe_ready_act, 2)
                elif n > XH:
                    pe.wait_ge(xe_ready_act, 2 * (n - XH + 1))
                for k, part in ((0, xn2_hi), (1, xn2_lo)):
                    mm(XE_PS[n][k][:, 0:PS], part[:, n, :], disp[:, n, :], start=True, stop=True).then_inc(xe_ps, 1)

            turn_x2(5)
            keep_busy(IDLE, 2)
            turn_x2(6)
            turn_x2(7)
            counts(0)
            for p in range(LATE, NP):
                logits(p)
            keep_busy(IDLE, 5)
            counts(1)
            keep_busy(IDLE, 4)
            for n in range(XH):
                dispatch(n)
            keep_busy(IDLE, 2)
            for n in range(XH, NP):
                dispatch(n)
            pe.wait_ge(xe_ready_act, 2 * XH + 2)
            keep_busy(p6, 2)

            def three_passes(out, lhs_hi, lhs_lo, rhs_hi, rhs_lo):
                mm(out, lhs_hi, rhs_hi, start=True, stop=False)
                mm(out, lhs_lo, rhs_hi, start=False, stop=False)
                return mm(out, lhs_hi, rhs_lo, start=False, stop=True)

            def up(m):
                e, c = divmod(m, FC)
                if m < 2:
                    pe.wait_ge(xe_ready_act, NP + XH)
                    pe.wait_ge(xe_ready_dve, XH)
                else:
                    pe.wait_ge(u_ready, m - 1)
                if c == 0:
                    pe.wait_ge(w_hi_ready, 2 * e + 2)
                    pe.wait_ge(w_lo_ready, 2 * e + 2)
                rhs_hi, rhs_lo = (t[:, e, :, :].rearrange("c n s -> c (n s)") for t in (xe_hi, xe_lo))
                for k in range(2):
                    last = three_passes(pS[m % 2][:, 512 * k:512 * k + ES], w_hi(e, k)[:, 128 * c:128 * c + 128],
                                        w_lo[:, e, k, 128 * c:128 * c + 128], rhs_hi, rhs_lo)
                last.then_inc(hg_ps, 1)

            def down(m):
                e, c = divmod(m, FC)
                pe.wait_ge(z_ready, m + 1)
                if c == 0 and e >= 1:
                    pe.wait_ge(oT_ready, e)
                last = mm(pT2[:, 0:ES], wp_sb[:, e, c, :], z[:, m % 3, :], start=(c == 0), stop=(c == FC - 1))
                if c == FC - 1:
                    last.then_inc(f_ps, 1)

            def turn_coll(i):
                gr, h = divmod(i, 2)
                e0, ne = GROUPS[gr]
                w = ne * SLOTS
                if i == 0:
                    pe.wait_ge(coll_ready, 8)
                else:
                    pe.wait_ge(collT_ready, i)
                for j in range(4):
                    last = nc.tensor.transpose(pT2[0:w, 512 + 128 * j:512 + 128 * j + 128],
                                               coll[:, 4 * h + j, e0 * SLOTS:e0 * SLOTS + w], ident[:, :])
                last.then_inc(cT2_ps, 1)

            def turn_out(i):
                gr, h = divmod(i, 2)
                e0, ne = GROUPS[gr]
                w = ne * SLOTS
                pe.wait_ge(collT_ready, 6)
                if 1 <= i < 5:
                    pe.wait_ge(os_ready, i)
                pe.wait_ge(oT_ready, e0 + ne)
                for j in range(4):
                    last = nc.tensor.transpose(OS_PS[i][0:w, 128 * j:128 * j + 128],
                                               oT[:, gr, 4 * h + j, 0:w], ident[:, :])
                last.then_inc(os_ps, 1)

            def collect(i):
                gr, h = divmod(i, 2)
                w = GROUPS[gr][1] * SLOTS
                if i < 5:
                    pe.wait_ge(os_ready, i + 1)
                else:
                    pe.wait_ge(os_ready_act, 1)
                for j in range(4):
                    last = mm((p6, p7)[h][:, 128 * j:128 * j + 128], collT[0:w, gr, 4 * h + j, :],
                              osl[0:w, i % 2, j, :], start=(gr == 0 and j == 0), stop=(gr == 2),
                              skip_group_check=True)
                last.then_inc(yf_ps, 1)

            M = E * FC
            for m in range(M + 2):
                if m < M:
                    up(m)
                if m >= 2:
                    down(m - 2)
                if m in TURN_COLL_AT:
                    turn_coll(TURN_COLL_AT.index(m))
                if m in COLLECT_AT:
                    collect(COLLECT_AT.index(m))
                if m in TURN_OUT_AT:
                    turn_out(TURN_OUT_AT.index(m))
            turn_out(4)
            pe.wait_ge(u_ready, E * FC)
            turn_out(5)
            collect(4)
            collect(5)

        @block.scalar
        def _(act):
            sc = nc.scalar
            for h in range(2):
                act.dma_start(c_sb[:, h * XH:(h + 1) * XH, :], c_v[:, h * XH:(h + 1) * XH, :]).then_inc(ld_ctx[h], 16)
            act.dma_start(wkv_sb[:, :], wkv).then_inc(ld_wkv, 16)
            act.dma_start(wq_sb[:, :], wq).then_inc(ld_wq, 16)
            act.wait_ge(c_ident, 1)
            sc.activation(warm[:, :], ident[:, 0:1], ACT.Exp)
            for h in range(2):
                act.wait_ge(cT_ps, h + 1)
                sc.activation(cT[:, 512 * h:512 * h + 512], pT2[:, 512 * h:512 * h + 512], ACT.Copy
                              ).then_inc(cT_ready, 1)
            act.wait_ge(xT_ps, 2)
            sc.activation(xnT[:, 512:1024], pT2[:, 512:1024], ACT.Copy).then_inc(xT_ready, 1)
            act.wait_ge(bT_ps, 1)
            sc.activation(bT[:, :], BANKS[0][:, 0:77], ACT.Copy).then_inc(bT_ready, 1)
            act.wait_ge(bT_ready, 1)
            act.wait_ge(k_ps, 1)
            sc.activation(ks[:, 0:512], BANKS[2], ACT.Identity, bias=bk_sb[:, 0:1]).then_inc(k_ready, 1)
            act.wait_ge(c_head, 1)
            act.wait_ge(k_ready, 2)
            for h in range(5, 8):
                sc.activation(kbd_v[:, h, :, 0, :], ks_v[:, :, 0, :], ACT.Copy, scale=hmask[:, h:h + 1]
                              ).then_inc(kbd_ready_act, 1)
            act.wait_ge(bqs_ready, 1)
            act.wait_ge(qbd_zero, 1)
            act.wait_ge(q_ps, 2)
            for h in range(2):
                for a in range(2):
                    q = slice(64 * a, 64 * a + 64)
                    sc.activation(qbd[q, 1, h * XH:h * XH + XH, a, :],
                                  p7[q, 256 * h:256 * h + 256].rearrange("p (n i) -> p n i", n=XH),
                                  ACT.Identity, bias=bqs[q, 1:2], scale=SCALE).then_inc(qbd_ready_act, 1)
            act.wait_ge(c_zero, 2)

            def values_in(t):
                act.wait_ge(v_ps, t + 1)
                src = pT2[:, 512 * t:512 * t + 512].rearrange("p (x q d) -> p x q d", q=2, d=D)
                dst = vbd[:, 2048 * t:2048 * t + 2048].rearrange("p (x w) -> p x w", w=64)
                for s in range(2):
                    for q in range(2):
                        at = 48 * q + 8 * s
                        sc.activation(dst[64 * s:64 * s + 64, :, at:at + 8], src[64 * s:64 * s + 64, :, q, :],
                                      ACT.Copy).then_inc(v_ready, 1)

            values_in(0)

            def later_keys(h):
                sc.activation(kbd_v[:, h, :, 1, :], ks_v[:, :, 1, :], ACT.Copy, scale=hmask[:, h:h + 1]
                              ).then_inc(kbd_ready_act, 1)

            act.wait_ge(ld_gate, 48)
            sc.activation(tgx[:, :], gx[:, :], ACT.Tanh).then_inc(tg_ready, 1)
            sc.activation(tgf[:, :], gf[:, :], ACT.Tanh).then_inc(tg_ready, 1)

            def exps(p):
                act.wait_ge(shifted, p + 1)
                sc.activation(pm[:, p % 2, :, :], pm[:, p % 2, :, :], ACT.Exp).then_inc(exped, 1)

            def x2T_out(p):
                act.wait_ge(x2T_ps, p + 1)
                sc.activation(xn2T[:, p, :], X2T_PS[p], ACT.Copy).then_inc(x2T_ready, 1)

            def probs_out(p):
                if p >= 2:
                    act.wait_ge(o_ps, p - 1)
                for h in range(2):
                    act.wait_ge(pT_ps, 2 * p + h + 1)
                    sc.activation(pT[:, p % 2, 512 * h:512 * h + 512], pT2[:, 512 * h:512 * h + 512],
                                  ACT.Copy).then_inc(pT_ready, 1)

            def round_w(u):
                e, k = divmod(u, 2)
                if k == 0:
                    act.wait_ge(ld_exp[e], 48)
                sc.activation(w_hi(e, k), w_raw[:, e, k, :], ACT.Copy).then_inc(w_hi_ready, 1)

            def round_x(h):
                pairs = slice(h * XH, (h + 1) * XH)
                if h == 0:
                    act.wait_ge(xn2_ready, XH)
                else:
                    act.wait_ge(xn2_ready, DVE_NORM)
                    act.wait_ge(xn2_late, NP - DVE_NORM)
                sc.activation(xn2_hi[:, pairs, :], xn2[:, pairs, :], ACT.Copy).then_inc(xn2_hi_ready, 1)

            done = 0
            for p in range(NP):
                if p == 1:
                    exps(1)
                if p >= 1:
                    probs_out(p - 1)
                if p >= 5:
                    x2T_out(p - 5)
                if p == 2:
                    later_keys(7)
                if p != 1:
                    exps(p)
                if p == 0:
                    values_in(1)
                if p == 1:
                    for h in (4, 5, 6):
                        later_keys(h)
                for u in range(done, ACT_UNITS[p]):
                    round_w(u)
                done = ACT_UNITS[p]
            probs_out(NP - 1)
            x2T_out(3)
            round_x(0)
            act.wait_ge(s_ps, NP)
            for u in range(done, 2 * E):
                round_w(u)
            x2T_out(4)
            x2T_out(5)
            x2T_out(6)
            x2T_out(7)
            round_x(1)

            def slots_in(n, k):
                act.wait_ge(xe_ps, 2 * n + k + 1)
                sc.activation((xe_hi, xe_lo)[k][:, :, n, :], XE_PS[n][k][:, 0:PS].rearrange("c (e s) -> c e s", e=E),
                              ACT.Copy).then_inc(xe_ready_act, 1)

            act.wait_ge(dl_ready, 1)
            sc.activation(ex[:, :], dl[:, :], ACT.Exp).then_inc(ex_ready, 1)
            act.wait_ge(tg_ready, 2)
            sc.activation(warm[:, :], tgf[:, :], ACT.Silu)
            for n in range(XH):
                slots_in(n, 0)
                slots_in(n, 1)
            for n in range(XH, NP):
                slots_in(n, 0)

            def hidden(m):
                e, c = divmod(m, FC)
                act.wait_ge(hg_ps, m + 1)
                if m >= 2:
                    act.wait_ge(u_ready, m - 1)
                sc.activation(hs[:, m % 2, :], pS[m % 2][:, 0:ES], ACT.Identity,
                              bias=bfc_sb[:, e, c:c + 1]).then_inc(h_ready, 1)

            def silu(m):
                act.wait_ge(u_ready, m + 1)
                sc.activation(z[:, m % 3, :], hg[:, m % 2, :], ACT.Silu).then_inc(z_ready, 1)

            def expert_out(e):
                gr = min(e // 3, 2)
                k = e - GROUPS[gr][0]
                act.wait_ge(f_ps, e + 1)
                sc.activation(oT[:, gr, :, k * SLOTS:(k + 1) * SLOTS],
                              pT2[:, 0:ES].rearrange("c (n s) -> c n s", n=NP), ACT.Identity,
                              bias=bp_sb[:, e:e + 1]).then_inc(oT_ready, 1)

            M = E * FC
            for m in range(M + 3):
                if m >= FC + 2 and m % FC == 2:
                    expert_out(m // FC - 1)
                if m < M:
                    hidden(m)
                if 1 <= m <= M:
                    silu(m - 1)
            w = GROUPS[2][1] * SLOTS
            act.wait_ge(os_ps, 6)
            act.wait_ge(yf_ps, 4)
            sc.activation(osl[0:w, 1, :, :].rearrange("s n c -> s (n c)"), OS_PS[5][0:w, :], ACT.Copy
                          ).then_inc(os_ready_act, 1)

        @block.vector
        def _(dve):
            v = nc.vector
            n = [0]

            def then(ins):
                link(dve, dve_chain, n, ins)

            def norm_stats(src, st, m_v, k):
                then(v.bn_stats(st[:, k, :], src[:, k, :]))
                return v.bn_aggr(m_v[:, k, :], st[:, k, :])

            v.memset(penalty[:, :, :], 0.0).then_inc(dve_chain, 1)
            n[0] += 1
            v.memset(qbd[:, :, :, :, :], 0.0).then_inc(qbd_zero, 1)
            for h in range(2):
                dve.wait_ge(ld_x[h], 16)
                for k in range(h * XH, (h + 1) * XH):
                    v.bn_stats(stats[:, k, :], x_sb[:, k, :]).then_inc(dve_chain, 1)
                n[0] += XH
                dve.wait_ge(dve_chain, n[0])
                for k in range(h * XH, (h + 1) * XH):
                    last = v.bn_aggr(mv[:, k, :], stats[:, k, :])
                    if k < (h + 1) * XH - 1:
                        last.then_inc(dve_chain, 1)
                        n[0] += 1
                last.then_inc(var_ready, 1)
            for h in range(2):
                dve.wait_ge(rstd_ready, h + 1)
                for k in range(h * XH, (h + 1) * XH):
                    last = v.tensor_scalar(xn[:, k, :], x_sb[:, k, :], mv[:, k, 0:1], rstd[:, k:k + 1],
                                           ALU.subtract, ALU.mult)
                last.then_inc(xn_ready, 1)
            dve.wait_ge(xT_ps, 1)
            v.tensor_copy(xnT[:, 0:512], pT2[:, 0:512]).then_inc(xT_ready, 1)
            dve.wait_ge(ld_mask, 64)
            for a in range(2):
                v.tensor_scalar(penalty[32 * a:32 * a + 1, :, :], mask_u8[32 * a:32 * a + 1, :, :], MASKED, None,
                                ALU.mult).then_inc(pen_ready, 1)
            dve.wait_ge(bT_ready, 1)
            v.tensor_scalar(bqs[:, :], bq_sb, SCALE, None, ALU.mult).then_inc(bqs_ready, 1)
            dve.wait_ge(k_ps, 2)
            v.tensor_scalar(ks[:, 512:1024], BANKS[3], bk_sb[:, 1:2], None, ALU.add).then_inc(k_ready, 1)
            dve.wait_ge(c_head, 1)
            dve.wait_ge(k_ready, 2)
            for h in range(0, 5):
                v.tensor_scalar(kbd_v[:, h, :, 0, :], ks_v[:, :, 0, :], hmask[:, h:h + 1], None, ALU.mult
                                ).then_inc(kbd_ready_dve, 1)
            dve.wait_ge(qbd_zero, 1)
            dve.wait_ge(q_ps, 1)
            for h in range(2):
                for a in range(2):
                    q = slice(64 * a, 64 * a + 64)
                    v.tensor_scalar(qbd[q, 0, h * XH:h * XH + XH, a, :],
                                    p6[q, 256 * h:256 * h + 256].rearrange("p (n i) -> p n i", n=XH),
                                    bq_sb[q, 0:1], SCALE, ALU.add, ALU.mult).then_inc(qbd_ready_dve, 1)
            v.tensor_copy(bvm[:, :], bv_sb.broadcast_to([C, P])).then_inc(bvm_ready, 1)
            then(v.tensor_reduce(nmask[:, :], mask_nat[:, :, :], AX_X, ALU.add))
            then(v.tensor_scalar(live[:, :], nmask[:, :], -1.0, float(T), ALU.mult, ALU.add))
            then(v.reciprocal(rlive[:, :], live[:, :]))
            then(v.tensor_tensor(nmask[:, :], live[:, :], rlive[:, :], ALU.mult))
            v.tensor_tensor(nanfix[:, :], nmask[:, :], nmask[:, :], ALU.subtract).then_inc(nan_ready, 1)

            def shift(p):
                dve.wait_ge(s_ps, p + 1)
                sv = pS[p % 2][:, :].rearrange("p (h j) -> p h j", h=H)
                then(v.tensor_reduce(negmax[:, p, :], sv, AX_X, ALU.max, negate=True))
                if p >= 2:
                    dve.wait_ge(pT_ps, 2 * (p - 1))
                v.tensor_tensor(pm[:, p % 2, :, :], sv, negmax[:, p, :].unsqueeze(2).broadcast_to([P, H, T]),
                                ALU.add).then_inc(shifted, 1)

            def attention_out(p):
                dve.wait_ge(o_ps, p + 1)
                then(v.reciprocal(rden[:, p % 2, :], O_PS[p][:, P:2 * P]))
                if p >= 2:
                    dve.wait_ge(y_ps, p - 1)
                v.tensor_tensor(aT[:, p % 2, :], O_PS[p][:, 0:P], rden[:, p % 2, :], ALU.mult).then_inc(aT_ready, 1)

            def normalise_late(p):
                dve.wait_ge(rstd2_late, p + 1 - DVE_NORM)
                v.tensor_scalar(xn2[:, p, :], x2[:, p, :], mv2[:, p, 0:1], rstd2[:, p:p + 1],
                                ALU.subtract, ALU.mult).then_inc(xn2_late, 1)

            def router_logits(g):
                both = slice(g * XH, (g + 1) * XH)
                dve.wait_ge(ld_router, 32)
                dve.wait_ge(lg_ps, (g + 1) * XH)
                src = p7[:, C:C + XH * E] if g == 0 else BANKS[2][:, 0:XH * E]
                v.tensor_tensor(lg[:, both, :], src.rearrange("p (n e) -> p n e", e=E),
                                rb_bc[:, :].unsqueeze(1).broadcast_to([P, XH, E]), ALU.add).then_inc(lg_read, 1)

            def best(g):
                pairs = range(g * XH, (g + 1) * XH)
                dve.wait_ge(lg_read, g + 1)
                for p in pairs:
                    v.max(mx[:, p, :], lg[:, p, :]).then_inc(dve_chain, 1)
                n[0] += XH
                dve.wait_ge(dve_chain, n[0])
                for p in pairs:
                    v.max_index(ix[:, p, :], mx[:, p, :], lg[:, p, :]).then_inc(dve_chain, 1)
                n[0] += XH

            def residual(p):
                if p == 0:
                    dve.wait_ge(xb_ready, 1)
                    dve.wait_ge(tg_ready, 2)
                dve.wait_ge(y_ps, p + 1)
                v.scalar_tensor_tensor(out=x2[:, p, :], in0=Y_PS[p], scalar=tgx[:, 0:1], in1=xb[:, p, :],
                                       op0=ALU.mult, op1=ALU.add).then_inc(x2_ready, 1)
                dve.wait_ge(x2_ready, p + 1)
                norm_stats(x2, stats2, mv2, p).then_inc(x2_stats, 1)

            for p in range(NP + 1):
                if p < NP:
                    shift(p)
                if p == 1:
                    dve.wait_ge(bvy_ps, 1)
                    dve.wait_ge(ld_gate, 48)
                    v.tensor_tensor(bias_y[:, :], p7[:, 0:C], bout_bc[:, :], ALU.add).then_inc(bias_y_ready, 1)
                if p >= 3:
                    residual(p - 3)
                if p >= 2:
                    attention_out(p - 2)

            def choices(g):
                pairs = slice(g * XH, (g + 1) * XH)
                dve.wait_ge(dve_chain, n[0])
                dve.wait_ge(c_route, 5)
                then(v.tensor_copy(idf[:, :, pairs].rearrange("p k n -> p n k"), ix[:, pairs, 0:2]))
                for k in range(2):
                    v.tensor_tensor(oh[:, k, pairs, :], iota_e[:, :].unsqueeze(1).broadcast_to([P, XH, E]),
                                    idf[:, k, pairs].unsqueeze(2).broadcast_to([P, XH, E]), ALU.is_equal
                                    ).then_inc(oh_ready, 1)

            def places(g):
                pairs = slice(g * XH, (g + 1) * XH)
                w = XH * E
                dve.wait_ge(pos_ps, g + 1)
                dve.wait_ge(oh_ready, 2 * g + 2)
                for k, pos in ((0, pos0), (1, pos1)):
                    v.scalar_tensor_tensor(out=pos[:, pairs, :].rearrange("p n e -> p (n e)"),
                                           in0=COUNT_PS[g][:, k * w:(k + 1) * w], scalar=1.0,
                                           in1=oh[:, k, pairs, :].rearrange("p n e -> p (n e)"),
                                           op0=ALU.add, op1=ALU.mult).then_inc(dve_chain, 1)
                n[0] += 2
                dve.wait_ge(dve_chain, n[0])
                then(v.tensor_tensor(slot[:, pairs, :], pos0[:, pairs, :], pos1[:, pairs, :], ALU.add))

            def dispatching(lo, hi, a):
                q = slice(64 * a, 64 * a + 64)
                dvw = disp[q, lo:hi, :].rearrange("p n (e a s) -> p (n e) a s", a=2, s=CAP)
                v.tensor_tensor(dvw[:, :, a, :],
                                slot[q, lo:hi, :].rearrange("p n e -> p (n e)").unsqueeze(2)
                                .broadcast_to([T, (hi - lo) * E, CAP]),
                                iota_s[q, :].unsqueeze(1).broadcast_to([T, (hi - lo) * E, CAP]), ALU.is_equal
                                ).then_inc(disp_ready, 1)

            router_logits(0)
            attention_out(NP - 1)
            residual(NP - 2)
            residual(NP - 1)
            normalise_late(5)
            normalise_late(6)
            best(0)
            normalise_late(7)
            choices(0)
            places(0)
            dve.wait_ge(disp_zero, 1)
            dispatching(0, XH, 0)
            router_logits(1)
            best(1)
            choices(1)
            v.tensor_tensor(dl[:, :], mx[:, :, 1], mx[:, :, 0], ALU.subtract).then_inc(dl_ready, 1)
            dispatching(0, XH, 1)
            places(1)
            for lo in (XH, XH + 2):
                for a in range(2):
                    dispatching(lo, lo + 2, a)
            for i in range(XH, NP):
                dve.wait_ge(xe_ps, 2 * i + 2)
                v.tensor_copy(xe_lo[:, :, i, :], XE_PS[i][1][:, 0:PS].rearrange("c (e s) -> c e s", e=E)
                              ).then_inc(xe_ready_dve, 1)

            def gate(m):
                e, c = divmod(m, FC)
                dve.wait_ge(h_ready, m + 1)
                if m >= 2:
                    dve.wait_ge(z_ready, m - 1)
                v.scalar_tensor_tensor(out=hg[:, m % 2, :], in0=pS[m % 2][:, 512:512 + ES],
                                       scalar=bg_sb[:, e, c:c + 1], in1=hs[:, m % 2, :],
                                       op0=ALU.add, op1=ALU.mult).then_inc(u_ready, 1)

            def coll_out(i):
                gr, h = divmod(i, 2)
                w = GROUPS[gr][1] * SLOTS
                dve.wait_ge(cT2_ps, i + 1)
                v.tensor_copy(collT[0:w, gr, 4 * h:4 * h + 4, :].rearrange("s n t -> s (n t)"),
                              pT2[0:w, 512:1024]).then_inc(collT_ready, 1)

            def slots_out(i):
                gr, h = divmod(i, 2)
                w = GROUPS[gr][1] * SLOTS
                dve.wait_ge(os_ps, i + 1)
                if i >= 2:
                    dve.wait_ge(yf_ps, i - 1)
                v.tensor_copy(osl[0:w, i % 2, :, :].rearrange("s n c -> s (n c)"),
                              OS_PS[i][0:w, :]).then_inc(os_ready, 1)

            def weights():
                dve.wait_ge(ex_ready, 1)
                then(v.tensor_scalar(den[:, :], ex[:, :], 1.0, None, ALU.add))
                then(v.reciprocal(pr[:, 0, :], den[:, :]))
                then(v.tensor_tensor(pr[:, 1, :], ex[:, :], pr[:, 0, :], ALU.mult))
                for k, w in ((0, pw0), (1, pw1)):
                    v.tensor_tensor(w[:, :, :], oh[:, k, :, :],
                                    pr[:, k, :].unsqueeze(2).broadcast_to([P, NP, E]), ALU.mult
                                    ).then_inc(dve_chain, 1)
                v.tensor_scalar(slotc[:, :, :], slot[:, :, :], float(CAP), None, ALU.min).then_inc(dve_chain, 1)
                n[0] += 3
                dve.wait_ge(dve_chain, n[0])
                then(v.tensor_tensor(pw[:, :, :], pw0[:, :, :], pw1[:, :, :], ALU.add))

            def reads_of(i):
                a, h = divmod(i, 2)
                q = slice(64 * a, 64 * a + 64)
                pairs = slice(h * XH, (h + 1) * XH)
                if i == 0:
                    dve.wait_ge(coll_zero, 1)
                cv = coll[q, pairs, :].rearrange("p n (e a s) -> p (n e) a s", a=2, s=CAP)[:, :, a, :]
                v.tensor_tensor(cv, slotc[q, pairs, :].rearrange("p n e -> p (n e)").unsqueeze(2)
                                .broadcast_to([T, XH * E, CAP]),
                                iota_s[q, :].unsqueeze(1).broadcast_to([T, XH * E, CAP]), ALU.is_equal
                                ).then_inc(slot_ready, 1)

            M = E * FC
            for m in range(M):
                gate(m)
                if m == 1:
                    weights()
                if 2 <= m < 6:
                    reads_of(m - 2)
                if m in TURN_COLL_AT:
                    coll_out(TURN_COLL_AT.index(m))
                if m in TURN_OUT_AT:
                    slots_out(TURN_OUT_AT.index(m))
            slots_out(4)
            for bank, base, lo, hi, collected in ((p6, 0, 0, 4, 5), (p7, 4, 4, 6, 6), (p7, 4, 6, 8, 6)):
                dve.wait_ge(yf_ps, collected)
                v.scalar_tensor_tensor(out=fin[:, lo:hi, :].rearrange("p n c -> p (n c)"),
                                       in0=bank[:, (lo - base) * C:(hi - base) * C], scalar=tgf[:, 0:1],
                                       in1=x2[:, lo:hi, :].rearrange("p n c -> p (n c)"),
                                       op0=ALU.mult, op1=ALU.add).then_inc(fin_ready, 1)


_INS = ["x", "ctx_1024", "mask_BxS2_bf0", "g_xattn", "g_ffn", "L0_xattn_Wq", "L0_xattn_bq", "L0_xattn_Wkv",
        "L0_xattn_bkv", "L0_xattn_Wout", "L0_xattn_bout", "L0_ffn_router_w", "L0_ffn_router_b",
        "L0_ffn_w_c_fc", "L0_ffn_b_c_fc", "L0_ffn_w_gate", "L0_ffn_b_gate", "L0_ffn_w_c_proj",
        "L0_ffn_b_c_proj"]
_OUTS = [((16, 64, 128), "float32")]


def kernel(**inputs):
    import numpy as _np
    import concourse.bacc as _bacc
    from concourse import mybir as _mybir
    from concourse.bass_utils import run_bass_kernel_spmd as _run

    nc = _bacc.Bacc("TRN2", target_bir_lowering=False, num_devices=1)
    arrays, args = {}, []
    for name in _INS:
        a = _np.ascontiguousarray(inputs[name])
        arrays[f"in_{name}_dram"] = a
        args.append(nc.dram_tensor(f"in_{name}_dram", a.shape, _mybir.dt.from_np(a.dtype), kind="ExternalInput").ap())
    for i, (shape, dtype) in enumerate(_OUTS):
        dt = _mybir.dt.from_np(_np.dtype(dtype))
        args.append(nc.dram_tensor(f"out_{i}_dram", shape, dt, kind="ExternalOutput").ap())
    gated_attention_moe(nc, *args)
    r = _run(nc, [arrays], core_ids=[0])
    got = tuple(r.results[0][f"out_{i}_dram"] for i in range(len(_OUTS)))
    return got[0]
```
